# Optimizing a Trainium2 kernel written in Bass

```python
import numpy as np
import jax
import jax.numpy as jnp

def _softmax(x, axis=-1):
    return jax.nn.softmax(x, axis=axis)

def _gelu(x):
    return jax.nn.gelu(x, approximate=True)

def _silu(x):
    return jax.nn.silu(x)

def _sigmoid(x):
    return jax.nn.sigmoid(x)

def _layernorm(x, axis=-1, eps=1e-05):
    m = jnp.mean(x, axis=axis, keepdims=True)
    v = jnp.var(x, axis=axis, keepdims=True)
    return (x - m) / jnp.sqrt(v + eps)

def _scatter_add(tgt, idx, src, axis=0):
    return tgt.at[idx].add(src)

def _segment_sum(src, seg, n):
    return jax.ops.segment_sum(src, seg, n)
kernel_name = 'mk_conv_preact_d4_conv_nhwc32_r2_df3bb2'

def setup_inputs(seed: int=0):
    np.random.seed(seed)
    _w = jnp.asarray

    def _rec_inputs():
        import jax
        import jax.numpy as jnp
        _gk = jax.random.key(seed)
        x = -0.0005207 + 1.001 * jax.random.normal(jax.random.fold_in(_gk, 1), (32, 32, 32, 32), jnp.float32)
        return x
    x = _rec_inputs()

    def _L0_conv_setup():
        import jax, jax.numpy as jnp
        import numpy as np
        EPS = 1e-05
        K = 3
        PAD = 1

        def binarize(x):
            scale = jnp.mean(jnp.abs(x))
            return jnp.sign(x) * scale
        key = jax.random.key(seed)
        k1, k2, k3 = jax.random.split(key, 3)
        B, Cin, Cout, H, W = (32, 32, 32, 32, 32)
        x = jax.random.normal(k1, (B, Cin, H, W), dtype=jnp.float32)
        weight = jax.random.normal(k2, (1, Cout, Cin, H, W, K * K), dtype=jnp.float32)
        bias_p = jax.random.normal(k3, (1, Cout, H, W), dtype=jnp.float32)
        gamma = jnp.ones((Cout,), dtype=jnp.float32)
        beta = jnp.zeros((Cout,), dtype=jnp.float32)
        return {'x': x, 'weight': weight, 'bias_p': bias_p, 'gamma': gamma, 'beta': beta}
    _L0_conv_all = _L0_conv_setup()
    _L0_conv_in = {k: v for k, v in _L0_conv_all.items() if k in ('weight', 'bias_p', 'gamma', 'beta')}
    del _L0_conv_all

    def _L1_conv_setup():
        import jax, jax.numpy as jnp
        import numpy as np
        KERNEL = 3
        PADDING = 1

        def _extract_patches(px, k):
            oh = px.shape[2] - k + 1
            ow = px.shape[3] - k + 1
            cols = [px[:, :, i:i + oh, j:j + ow] for i in range(k) for j in range(k)]
            p = jnp.stack(cols, axis=-1)
            return p.reshape(p.shape[:-1] + (k, k))
        key = jax.random.key(seed)
        k1, k2 = jax.random.split(key)
        x = jax.random.normal(k1, (32, 32, 32, 32), dtype=jnp.float32)
        weights = jax.random.uniform(k2, (32, 32, 32, 32, KERNEL, KERNEL), dtype=jnp.float32)
        return {'x': x, 'weights': weights}
    _L1_conv_all = _L1_conv_setup()
    _L1_conv_in = {k: v for k, v in _L1_conv_all.items() if k in ('weights',)}
    del _L1_conv_all

    def _L2_conv_setup():
        import jax, jax.numpy as jnp
        import numpy as np
        EPS = 1e-05
        K = 3
        PAD = 1

        def binarize(x):
            scale = jnp.mean(jnp.abs(x))
            return jnp.sign(x) * scale
        key = jax.random.key(seed)
        k1, k2, k3 = jax.random.split(key, 3)
        B, Cin, Cout, H, W = (32, 32, 32, 32, 32)
        x = jax.random.normal(k1, (B, Cin, H, W), dtype=jnp.float32)
        weight = jax.random.normal(k2, (1, Cout, Cin, H, W, K * K), dtype=jnp.float32)
        bias_p = jax.random.normal(k3, (1, Cout, H, W), dtype=jnp.float32)
        gamma = jnp.ones((Cout,), dtype=jnp.float32)
        beta = jnp.zeros((Cout,), dtype=jnp.float32)
        return {'x': x, 'weight': weight, 'bias_p': bias_p, 'gamma': gamma, 'beta': beta}
    _L2_conv_all = _L2_conv_setup()
    _L2_conv_in = {k: v for k, v in _L2_conv_all.items() if k in ('weight', 'bias_p', 'gamma', 'beta')}
    del _L2_conv_all

    def _L3_conv_setup():
        import jax, jax.numpy as jnp
        import numpy as np
        B, C, H = (32, 32, 32)

        def _pm_cross_pairs(ks):
            a, b = ([], [])
            for j in range(1, ks):
                for i in range(ks - j):
                    a.append(i)
                    b.append(i + j)
            return (np.array(a, dtype=np.int32), np.array(b, dtype=np.int32))
        key = jax.random.key(seed)
        k1, k2 = jax.random.split(key)
        ia, ib = _pm_cross_pairs(H)
        hk = ia.shape[0] + 2 * H
        x = jax.random.normal(k1, (B, C, H, H), dtype=jnp.float32)
        weight = 0.1 * jax.random.normal(k2, (C, H, hk, H), dtype=jnp.float32)
        return {'x': x, 'weight': weight, 'idx_a': jnp.asarray(ia), 'idx_b': jnp.asarray(ib)}
    _L3_conv_all = _L3_conv_setup()
    _L3_conv_in = {k: v for k, v in _L3_conv_all.items() if k in ('weight', 'idx_a', 'idx_b')}
    del _L3_conv_all
    return {'x': x, 'L0_conv_weight': _L0_conv_in['weight'], 'L0_conv_bias_p': _L0_conv_in['bias_p'], 'L0_conv_gamma': _L0_conv_in['gamma'], 'L0_conv_beta': _L0_conv_in['beta'], 'L1_conv_weights': _L1_conv_in['weights'], 'L2_conv_weight': _L2_conv_in['weight'], 'L2_conv_bias_p': _L2_conv_in['bias_p'], 'L2_conv_gamma': _L2_conv_in['gamma'], 'L2_conv_beta': _L2_conv_in['beta'], 'L3_conv_weight': _L3_conv_in['weight'], 'L3_conv_idx_a': _L3_conv_in['idx_a'], 'L3_conv_idx_b': _L3_conv_in['idx_b']}

def reference(x, L0_conv_weight, L0_conv_bias_p, L0_conv_gamma, L0_conv_beta, L1_conv_weights, L2_conv_weight, L2_conv_bias_p, L2_conv_gamma, L2_conv_beta, L3_conv_weight, L3_conv_idx_a, L3_conv_idx_b):
    import jax
    import jax.numpy as jnp

    def _L0_conv_ref(x, weight, bias_p, gamma, beta):
        import jax, jax.numpy as jnp
        import numpy as np
        EPS = 1e-05
        K = 3
        PAD = 1

        def binarize(x):
            scale = jnp.mean(jnp.abs(x))
            return jnp.sign(x) * scale
        B, C, H, W = x.shape
        xp = jnp.pad(x, ((0, 0), (0, 0), (PAD, PAD), (PAD, PAD)))
        patches = jnp.stack([xp[:, :, i:i + H, j:j + W] for i in range(K) for j in range(K)], axis=-1)
        wb = binarize(weight)[0]
        out = jnp.einsum('bchwk,ochwk->bohw', patches, wb)
        out = out + bias_p
        mean = out.mean(axis=(0, 2, 3), keepdims=True)
        var = out.var(axis=(0, 2, 3), keepdims=True)
        out = gamma[None, :, None, None] * (out - mean) * jax.lax.rsqrt(var + EPS) + beta[None, :, None, None]
        out = jax.nn.relu(out)
        return binarize(out)

    def _L1_conv_ref(x, weights):
        import jax, jax.numpy as jnp
        import numpy as np
        KERNEL = 3
        PADDING = 1

        def _extract_patches(px, k):
            oh = px.shape[2] - k + 1
            ow = px.shape[3] - k + 1
            cols = [px[:, :, i:i + oh, j:j + ow] for i in range(k) for j in range(k)]
            p = jnp.stack(cols, axis=-1)
            return p.reshape(p.shape[:-1] + (k, k))
        px = jnp.pad(x, ((0, 0), (0, 0), (PADDING, PADDING), (PADDING, PADDING)))
        patches = _extract_patches(px, KERNEL)
        out = jnp.einsum('bcwhij,hwocij->bohw', patches, weights)
        return out

    def _L2_conv_ref(x, weight, bias_p, gamma, beta):
        import jax, jax.numpy as jnp
        import numpy as np
        EPS = 1e-05
        K = 3
        PAD = 1

        def binarize(x):
            scale = jnp.mean(jnp.abs(x))
            return jnp.sign(x) * scale
        B, C, H, W = x.shape
        xp = jnp.pad(x, ((0, 0), (0, 0), (PAD, PAD), (PAD, PAD)))
        patches = jnp.stack([xp[:, :, i:i + H, j:j + W] for i in range(K) for j in range(K)], axis=-1)
        wb = binarize(weight)[0]
        out = jnp.einsum('bchwk,ochwk->bohw', patches, wb)
        out = out + bias_p
        mean = out.mean(axis=(0, 2, 3), keepdims=True)
        var = out.var(axis=(0, 2, 3), keepdims=True)
        out = gamma[None, :, None, None] * (out - mean) * jax.lax.rsqrt(var + EPS) + beta[None, :, None, None]
        out = jax.nn.relu(out)
        return binarize(out)

    def _L3_conv_ref(x, weight, idx_a, idx_b):
        import jax, jax.numpy as jnp
        import numpy as np
        B, C, H = (32, 32, 32)

        def _pm_cross_pairs(ks):
            a, b = ([], [])
            for j in range(1, ks):
                for i in range(ks - j):
                    a.append(i)
                    b.append(i + j)
            return (np.array(a, dtype=np.int32), np.array(b, dtype=np.int32))
        cross = x[..., idx_a] * x[..., idx_b]
        feat = jnp.concatenate([x, x * x, cross], axis=-1)
        return jnp.einsum('bcij,cijo->bcio', feat, weight)

    def _gn(v, G=16, eps=1e-05):
        B_, H_, W_, C_ = v.shape
        g = v.reshape(B_, H_, W_, G, C_ // G)
        m = jnp.mean(g, axis=(1, 2, 4), keepdims=True)
        s = jnp.var(g, axis=(1, 2, 4), keepdims=True)
        return ((g - m) / jnp.sqrt(s + eps)).reshape(v.shape)

    def _ln_c(v, eps=1e-06):
        m = jnp.mean(v, axis=-1, keepdims=True)
        s = jnp.var(v, axis=-1, keepdims=True)
        return (v - m) / jnp.sqrt(s + eps)

    def _ln_t(v, eps=1e-05):
        m = jnp.mean(v, axis=-1, keepdims=True)
        s = jnp.var(v, axis=-1, keepdims=True)
        return (v - m) / jnp.sqrt(s + eps)

    def _to_tokens(v):
        B_, H_, W_, C_ = v.shape
        return v.reshape(B_, H_ * W_, C_)

    def _from_tokens(t, like):
        return t.reshape(like.shape)
    x = x + _L0_conv_ref(_gn(x), L0_conv_weight, L0_conv_bias_p, L0_conv_gamma, L0_conv_beta)
    x = x + _L1_conv_ref(_gn(x), L1_conv_weights)
    x = x + _L2_conv_ref(_gn(x), L2_conv_weight, L2_conv_bias_p, L2_conv_gamma, L2_conv_beta)
    x = x + _L3_conv_ref(_gn(x), L3_conv_weight, L3_conv_idx_a, L3_conv_idx_b)
    return x

_drawn_inputs = setup_inputs


def setup_inputs(seed=0):
    import zlib

    import numpy as np

    out = dict(_drawn_inputs(seed))
    spreads = {'L0_conv_gamma': (1.0, 0.2),
     'L0_conv_beta': (0.0, 0.1),
     'L2_conv_gamma': (1.0, 0.6),
     'L2_conv_beta': (0.0, 2.0)}
    factors = {'L2_conv_bias_p': 25.5}
    for name, (base, spread) in spreads.items():
        noise = np.random.default_rng([zlib.crc32(name.encode()), seed]).standard_normal(out[name].shape)
        drawn = base * np.exp(spread * noise) if base else spread * noise
        out[name] = jnp.asarray(drawn.astype(out[name].dtype))
    for name, factor in factors.items():
        out[name] = (out[name] * factor).astype(out[name].dtype)
    return out
```

```python
from contextlib import ExitStack

import concourse.bass as bass
from concourse import mybir

F32 = mybir.dt.float32
F16 = mybir.dt.float16
BF16 = mybir.dt.bfloat16
I32 = mybir.dt.int32
ALU = mybir.AluOpType
ACT = mybir.ActivationFunctionType
X = mybir.AxisListType.X

P = 128
B = C = H = W = 32
G = 4
V = 32 // G
U = 32
ROW = V * B
STATE = U * ROW
TAPS = 3
KC = TAPS * C
CHUNK = V * G * TAPS * C
PAD = U + 2
SLOTS = V + 2
UC = 2
RING = 4
NCHUNK = 4
CU = U // NCHUNK
GN_COUNT = C * H * 2
BN_COUNT = B * H * W
GN_EPS = 1e-5
BN_EPS = 1e-5
HALF_SCALE = 1024.0

PAIRS = W * (W - 1) // 2
FEATS = 2 * W + PAIRS
FT = 5
FP = FEATS // FT
C4 = 4
NK = V * C // C4
POS = G * C4
FCOL = POS * B
W3CHUNK = FT * POS * W


def build(nc, x, w_conv, bias, gamma_beta, w_mix, mats, sel_rows, sel_index, is_linear, out):
    ctx = ExitStack()
    with ctx:
        def sb(name, shape, dt):
            return ctx.enter_context(nc.sbuf_tensor(name, shape, dt))

        def sem(name):
            return ctx.enter_context(nc.semaphore(name))

        def sems(name, n):
            return [sem(f"{name}{i}") for i in range(n)]

        state_a = sb("state_a", [P, STATE], F32)
        state_b = sb("state_b", [P, STATE], F32)
        work = sb("work", [P, 2 * STATE], F32)
        norm = work[:, 0:STATE]
        norm16 = norm.bitcast(F16)
        WIN = G * UC * SLOTS * B
        window = [work[0:KC, STATE + n * WIN:STATE + (n + 1) * WIN] for n in range(2)]
        zeros = work[0:C, STATE:STATE + PAD * B]
        sel_i = work[0:KC, 0:2 * FEATS].bitcast(I32).rearrange("p (s n) -> p s n", s=2)
        wring = sb("wring", [P, RING, CHUNK], F32)
        signs = sb("signs", [P, 2, CHUNK], F16)
        bias_sb = [sb(f"bias{m}", [P, U * V], F32) for m in range(2)]
        gb_sb = sb("gb_sb", [P, 4], F32)
        mats_sb = sb("mats_sb", [P, 4, P], F32)
        in_quadrant, everywhere, same_channel, same_pair = (mats_sb[:, n, :] for n in range(4))
        red = sb("red", [P, 2, 512], F32)
        mean = sb("mean", [P, 512], F32)
        rstd = sb("rstd", [P, 512], F32)
        tmp_a = sb("tmp_a", [P, 512], F32)
        tmp_b = sb("tmp_b", [P, 512], F32)
        abs_sums = sb("abs_sums", [P, U], F32)
        abs_sum = sb("abs_sum", [P, 1], F32)
        sc = sb("sc", [P, 16], F32)
        bst = sb("bst", [P, STATE // 512, 6], F32)
        relu_sums = sb("relu_sums", [P, NCHUNK], F32)
        sel = sb("sel", [KC, 2, FEATS], BF16)
        row_id = sb("row_id", [KC, 1], F32)
        linear = sb("linear", [FP, FT], F32)
        parts = work[0:KC, :].bitcast(BF16).rearrange("p (g n) -> p g n", g=G)
        feats = [state_b[0:FP, n * FT * FCOL:(n + 1) * FT * FCOL].rearrange("p (t n) -> p t n", t=FT) for n in range(2)]
        xn = [state_b[:, i * 1024:(i + 1) * 1024] for i in range(V)]
        thirds = signs[:, :, :].bitcast(BF16).rearrange("p s (k n) -> p s k n", k=3)
        left = state_b[0:FP, 7168:7168 + 2 * FCOL].rearrange("p (s n) -> p s n", s=2)

        psum = ctx.enter_context(nc.psum_tensor("psum", [P, 8, 512], F32))

        image = nc.dram_tensor("image", (C, PAD, PAD, B), I32, kind="Internal").ap()
        parts_dram = nc.dram_tensor("parts_dram", (G, W, 3, V, C * B), BF16, kind="Internal").ap()

        x_in = sem("x_in")
        consts_in = sem("consts_in")
        zeros_set = sem("zeros_set")
        border_in = sem("border_in")
        sel_made = sem("sel_made")
        w_in = sems("w_in", RING)
        signs_made = sem("signs_made")
        abs_made = sem("abs_made")
        conv_done = sem("conv_done")
        bank_free = sem("bank_free")
        window_in = sems("window_in", 2)
        image_in = [sems(f"image_in{l}_", NCHUNK) for l in range(3)]
        squares = sems("squares", 4)
        gn_red = sems("gn_red", 4)
        gn_sums = sems("gn_sums", 4)
        xn_made = sems("xn_made", 4)
        hi_made = sems("hi_made", 3)
        norm_made = sems("norm_made", 3)
        state_done = sems("state_done", 4)
        abs_red = sems("abs_red", 2)
        abs_total = sems("abs_total", 2)
        bn_mean_in = sems("bn_mean_in", 2)
        bn_mean = sems("bn_mean", 2)
        bn_var_in = sems("bn_var_in", 2)
        bn_var = sems("bn_var", 2)
        bn_affine = sems("bn_affine", 2)
        relu_made = sems("relu_made", 2)
        relu_red = sems("relu_red", 2)
        relu_total = sems("relu_total", 2)
        inverse = sem("inverse")
        root = sem("root")
        dve_chain = sem("dve_chain")
        act_chain = sem("act_chain")
        transposed = sem("transposed")
        t_hi = sem("t_hi")
        t_rest = sem("t_rest")
        t_mid = sem("t_mid")
        t_lo = sem("t_lo")
        parts_out = sems("parts_out", 2)
        parts_in = sem("parts_in")
        gathered = sem("gathered")
        left_made = sem("left_made")
        feats_made = sem("feats_made")
        mixed = sem("mixed")
        result_made = sem("result_made")
        out_sem = sem("out_sem")

        block = ctx.enter_context(nc.Block())

        states = [(state_a, state_b), (state_a, state_b), (state_b, state_a)]

        def rows(t, c):
            return t[:, c * CU * ROW:(c + 1) * CU * ROW]

        @block.sync
        def _(sp):
            def load_weights(layer, u, slot):
                if layer < 3:
                    sp.dma_start(wring[0:KC, slot, :], w_conv[layer][u]).then_inc(w_in[slot], 16)
                else:
                    sp.dma_start(wring[0:FP, slot, 0:W3CHUNK], w_mix[u]).then_inc(w_in[slot], 16)

            def load_window(n, u):
                dst = window[n].bitcast(I32).rearrange("p (g u n) -> p g u n", g=G, u=UC)
                for tap in range(TAPS):
                    src = image[:, bass.ds(u + tap, UC), :, :]
                    for g in range(G):
                        sp.dma_start(dst[tap * C:(tap + 1) * C, g, :, :],
                                     src[:, :, g * V:g * V + SLOTS, :].rearrange("c u s b -> c u (s b)")
                                     ).then_inc(window_in[n], 16)

            for c in range(NCHUNK):
                sp.dma_start(rows(state_a, c), rows(x, c)).then_inc(x_in, 16)
            for s in range(RING):
                load_weights(0, s, s)
            sp.wait_ge(zeros_set, 1)
            zi = zeros.bitcast(I32)
            for edge in (0, PAD - 1):
                sp.dma_start(image[:, edge, :, :].rearrange("c v b -> c (v b)"), zi).then_inc(border_in, 16)
                sp.dma_start(image[:, 1:PAD - 1, edge, :],
                             zi[:, 0:U * B].rearrange("c (u b) -> c u b", u=U)).then_inc(border_in, 16)
            sp.wait_ge(border_in, 64)
            for layer in range(3):
                ni = norm.bitcast(I32).rearrange("p (u n) -> p u n", u=U)
                if layer:
                    for n in range(2):
                        sp.wait_ge(window_in[n], 16 * TAPS * G * 8 * layer)
                for c in range(NCHUNK):
                    sp.wait_ge(norm_made[layer], c + 1)
                    for g in range(G):
                        sp.dma_start(image[:, 1 + c * CU:1 + (c + 1) * CU, 1 + g * V:1 + (g + 1) * V, :]
                                     .rearrange("c u v b -> c u (v b)"),
                                     ni[g * C:(g + 1) * C, c * CU:(c + 1) * CU, :]).then_inc(image_in[layer][c], 16)
                for c in range(NCHUNK):
                    sp.wait_ge(image_in[layer][c], 16 * G)
                if layer:
                    sp.wait_ge(conv_done, U * layer)
                load_window(0, 0)
                load_window(1, UC)

                def slot_used(u):
                    if layer == 1:
                        sp.wait_ge(conv_done, U * layer + u + 1)
                    else:
                        sp.wait_ge(signs_made, U * (layer // 2) + u + 1)
                        sp.wait_ge(abs_made, U * (layer // 2) + u + 1)

                with sp.Fori(0, U // RING - 1) as it:
                    for s in range(RING):
                        slot_used(it * RING + s)
                        load_weights(layer, it * RING + s + RING, s)
                        if s % 2:
                            sp.wait_ge(conv_done, it * RING + (U * layer + s + 1))
                            load_window(s // 2, it * RING + s + 1 + UC)
                for s in range(RING):
                    slot_used(U - RING + s)
                    load_weights(layer + 1, s, s)

            def load_mix(k, slot):
                sp.wait_ge(mixed, k + (1 - RING))
                load_weights(3, k, slot)

            for i in range(V):
                n = i % 2
                sp.wait_ge(t_lo, i + 1)
                sp.dma_start(parts_dram[:, :, :, i, :].rearrange("g w k n -> (g w) k n"),
                             thirds[:, n, :, :]).then_inc(parts_out[n], 16)
                sp.wait_ge(parts_out[n], 16 * (i // 2 + 1))
                for k in range(3):
                    sp.dma_start(parts[k * W:(k + 1) * W, :, i * C * B:(i + 1) * C * B],
                                 parts_dram[:, :, k, i, :].rearrange("g w n -> w g n")).then_inc(parts_in, 16)
            with sp.Fori(1, NK // RING) as it:
                for s in range(RING):
                    load_mix(it * RING + s, s)

        @block.gpsimd
        def _(pool):
            pool.memset(zeros, 0.0).then_inc(zeros_set, 1)
            for n, (dst, src) in enumerate([(mats_sb[:, :, :], mats), (gb_sb[:, :], gamma_beta),
                                            (bias_sb[0][:, :], bias[0]), (bias_sb[1][:, :], bias[1]),
                                            (sel_i, sel_index), (row_id[:, :], sel_rows),
                                            (linear[:, :], is_linear)]):
                pool.dma_start(dst, src).then_inc(consts_in, 16)
            with pool.Fori(0, NK // 4) as it:
                pool.wait_ge(result_made, it * 4 + 4)
                pool.dma_start(out[:, bass.ds(it * 512, 512)], state_a[:, bass.ds(it * 512, 512)]).then_inc(out_sem, 16)
            pool.wait_ge(out_sem, 16 * (NK // 4))

        CONSTS = 16 * 7

        @block.scalar
        def _(act):
            chain = [0]

            def link(ins):
                chain[0] += 1
                ins.then_inc(act_chain, 1)

            def square(layer):
                st, scratch = states[layer]
                for c in range(NCHUNK):
                    if layer == 0:
                        act.wait_ge(x_in, 64)
                    else:
                        act.wait_ge(*(state_done[0], c + 1) if layer == 1 else (bank_free, RING + 2 * U))
                    act.activation(rows(scratch, c), rows(st, c), ACT.Square).then_inc(squares[layer], 1)

            def take_root(out, inv, nth):
                act.wait_ge(inverse, nth)
                act.activation(out, inv, ACT.Sqrt).then_inc(root, 1)

            for layer in range(3):
                st, scratch = states[layer]
                square(layer)
                n_stat = ROW if layer < 2 else 512
                take_root(rstd[:, 0:n_stat], tmp_a[:, 0:n_stat], 2 * layer + 1 - layer // 2)
                if layer == 1:
                    continue
                m = layer // 2
                hi = norm16.rearrange("p (u v k b) -> p u v k b", u=U, v=V, k=2)[:, :, :, 0, :]
                t = scratch[:, :].rearrange("p (u v b) -> p u v b", u=U, v=V)
                for c in range(NCHUNK):
                    act.wait_ge(xn_made[layer], c + 1)
                    for h in range(2):
                        us = slice(c * CU + h * CU // 2, c * CU + (h + 1) * CU // 2)
                        act.activation(hi[:, us], t[:, us], ACT.Copy).then_inc(hi_made[layer], 1)
                for u in range(2):
                    act.wait_ge(w_in[u], 16 * (8 * layer + 1))
                    if m:
                        act.wait_ge(conv_done, U * layer)
                    act.activation(signs[0:KC, u, :], wring[0:KC, u, :], ACT.Sign).then_inc(signs_made, 1)
                for u in range(2, RING):
                    act.wait_ge(w_in[u], 16 * (8 * layer + 1))
                    act.wait_ge(conv_done, U * layer + u - 1)
                    act.activation(signs[0:KC, u % 2, :], wring[0:KC, u, :], ACT.Sign).then_inc(signs_made, 1)
                with act.Fori(1, U // RING) as it:
                    for s in range(RING):
                        act.wait_ge(w_in[s], it * 16 + 16 * (8 * layer + 1))
                        act.wait_ge(conv_done, it * RING + (U * layer + s - 1))
                        act.activation(signs[0:KC, s % 2, :], wring[0:KC, s, :], ACT.Sign).then_inc(signs_made, 1)
                take_root(sc[:, 11:12], sc[:, 15:16], 2 + 3 * m)
                act.wait_ge(bn_affine[m], 2)
                for c in range(NCHUNK):
                    act.activation(rows(scratch, c), rows(scratch, c), ACT.Relu, scale=sc[:, 4:5], bias=sc[:, 5:6],
                                   accum_out=relu_sums[:, c:c + 1]).then_inc(relu_made[m], 1)

            for i in range(V):
                act.wait_ge(transposed, i + 1)
                act.activation(norm[:, i * 1024:(i + 1) * 1024], state_a[:, i * 1024:(i + 1) * 1024],
                               ACT.Square).then_inc(squares[3], 1)
            take_root(rstd[:, 0:B], tmp_a[:, 0:B], 6)
            for i in range(V):
                n = i % 2
                act.wait_ge(xn_made[3], i + 1)
                if i >= 2:
                    act.wait_ge(parts_out[n], 16 * (i // 2))
                act.activation(thirds[:, n, 0, :], xn[i], ACT.Copy).then_inc(t_hi, 1)
                act.wait_ge(t_rest, i + 1)
                act.activation(thirds[:, n, 1, :], xn[i], ACT.Copy).then_inc(t_mid, 1)
            with act.Fori(0, NK // 2) as it:
                for g in range(2 * FT):
                    act.wait_ge(gathered, it * (2 * FT) + g + 1)
                    act.activation(left[:, g % 2, :], psum[0:FP, 2 + g % 2, :], ACT.Copy).then_inc(left_made, 1)

        @block.vector
        def _(dve):
            chain = [0]

            def link(ins):
                chain[0] += 1
                ins.then_inc(dve_chain, 1)
                dve.wait_ge(dve_chain, chain[0])

            def inverse_root(out, var, tmp, eps, nth):
                link(dve.tensor_scalar(var, var, eps, None, ALU.add))
                dve.reciprocal(tmp, var).then_inc(inverse, 1)
                dve.wait_ge(root, nth)
                link(dve.tensor_tensor(tmp, out, out, ALU.mult))
                link(dve.tensor_tensor(tmp, tmp, var, ALU.mult))
                link(dve.tensor_scalar(tmp, tmp, -0.5, 1.5, ALU.mult, ALU.add))
                link(dve.tensor_tensor(out, out, tmp, ALU.mult))

            dve.memset(sc[:, :], 0.0).then_inc(bank_free, RING)
            dve.wait_ge(consts_in, CONSTS)
            for side in range(2):
                dve.tensor_scalar(sel[:, side, :], sel_i[:, side, :], row_id[:, 0:1], None,
                                  ALU.is_equal).then_inc(sel_made, 1)

            def pairs_of_v(t):
                return t.rearrange("p (u r) -> p r u", r=ROW)

            def pairs_of_u(t):
                return t.rearrange("p (u k b) -> p u b k", u=U // 2, b=B)

            for layer in range(3):
                st, scratch = states[layer]
                by_v = layer < 2
                n_stat = ROW if by_v else 512
                def reduce(side, t):
                    if by_v:
                        dve.tensor_reduce(red[:, side, 0:ROW], pairs_of_v(t), X, ALU.add).then_inc(gn_red[layer], 1)
                    else:
                        dve.tensor_reduce(red[:, side, :].rearrange("p (u b) -> p u b", b=B), pairs_of_u(t), X,
                                          ALU.add).then_inc(gn_red[layer], 1)
                if layer == 0:
                    dve.wait_ge(x_in, 64)
                elif layer == 1:
                    dve.wait_ge(state_done[0], NCHUNK)
                else:
                    dve.wait_ge(bank_free, RING + 2 * U)
                reduce(0, st[:, :])
                dve.wait_ge(squares[layer], NCHUNK)
                reduce(1, scratch[:, :])
                dve.wait_ge(gn_sums[layer], 1)
                sums = psum[:, 4, 0:n_stat]
                sums2 = psum[:, 5, 0:n_stat]
                mn, rs, ta, tb = (t[:, 0:n_stat] for t in (mean, rstd, tmp_a, tmp_b))
                link(dve.tensor_scalar(mn, sums, 1.0 / GN_COUNT, None, ALU.mult))
                link(dve.tensor_tensor(ta, mn, mn, ALU.mult))
                link(dve.scalar_tensor_tensor(tb, sums2, 1.0 / GN_COUNT, ta, ALU.mult, ALU.subtract))
                inverse_root(rs, tb, ta, GN_EPS, 2 * layer + 1 - layer // 2)
                if layer != 1:
                    link(dve.tensor_scalar(rs, rs, HALF_SCALE, None, ALU.mult))
                dst = norm if layer == 1 else scratch
                for c in range(NCHUNK):
                    if by_v:
                        view = [rows(t, c).rearrange("p (u r) -> p u r", r=ROW) for t in (st, dst)]
                        m_op, r_op = (t.unsqueeze(1).to_broadcast([P, CU, ROW]) for t in (mn, rs))
                    else:
                        view = [rows(t, c).rearrange("p (u k b) -> p u k b", u=CU // 2, b=B) for t in (st, dst)]
                        m_op, r_op = (t[:, c * CU // 2 * B:(c + 1) * CU // 2 * B].rearrange("p (u b) -> p u b", b=B)
                                      .unsqueeze(2).to_broadcast([P, CU // 2, 2 * V, B]) for t in (mn, rs))
                    link(dve.tensor_tensor(view[1], view[0], m_op, ALU.subtract))
                    dve.tensor_tensor(view[1], view[1], r_op, ALU.mult).then_inc(
                        norm_made[1] if layer == 1 else xn_made[layer], 1)
                if layer != 1:
                    halves = norm16.rearrange("p (u v k b) -> p u v k b", u=U, v=V, k=2)
                    t = scratch[:, :].rearrange("p (u v b) -> p u v b", u=U, v=V)
                    for c in range(NCHUNK):
                        dve.wait_ge(xn_made[layer], c + 1)
                        dve.wait_ge(hi_made[layer], 2 * (c + 1))
                        for h in range(2):
                            us = slice(c * CU + h * CU // 2, c * CU + (h + 1) * CU // 2)
                            last = dve.tensor_tensor(halves[:, us, :, 1, :], t[:, us], halves[:, us, :, 0, :],
                                                     ALU.subtract)
                        last.then_inc(norm_made[layer], 1)

                if layer == 1:
                    src = st[:, :].rearrange("p (h v b) -> p h v b", h=H, b=B)
                    for wg in range(G):
                        with dve.Fori(0, V // RING) as half:
                            for s in range(RING):
                                dve.wait_ge(conv_done, half * RING + (U * layer + wg * V + s + 1))
                                for g in range(G):
                                    res = scratch[g * C:(g + 1) * C, bass.ds((half * RING + (wg * V + s)) * ROW, ROW)]
                                    old = src[wg * C:(wg + 1) * C, g * V:(g + 1) * V, bass.ds(half * RING + s, 1), :]
                                    last = dve.tensor_tensor(
                                        res.rearrange("p (v b) -> p v b", b=B),
                                        psum[g * C:(g + 1) * C, s, 0:ROW].rearrange("p (v b) -> p v b", b=B),
                                        old.rearrange("p v o b -> p v (o b)"), ALU.add)
                                last.then_inc(bank_free, 1)
                    continue

                m = layer // 2
                with dve.Fori(0, U // RING) as it:
                    for s in range(RING):
                        dve.wait_ge(w_in[s], it * 16 + 16 * (8 * layer + 1))
                        dve.tensor_reduce(abs_sums[0:KC, bass.ds(it * RING + s, 1)], wring[0:KC, s, :], X, ALU.add,
                                          apply_absolute_value=True).then_inc(abs_made, 1)
                        dve.wait_ge(conv_done, it * RING + (U * layer + s + 1))
                        dve.tensor_reduce(
                            scratch[:, bass.ds((it * RING + s) * ROW, ROW)].rearrange("p (v b) -> p v b", b=B),
                            psum[:, s, :].rearrange("p (v k b) -> p v b k", k=2, b=B), X, ALU.add
                        ).then_inc(bank_free, 1)
                dve.wait_ge(abs_made, U * (m + 1))
                dve.tensor_reduce(abs_sum[0:KC, :], abs_sums[0:KC, :], X, ALU.add).then_inc(abs_red[m], 1)
                dve.wait_ge(abs_total[m], 1)
                link(dve.tensor_scalar(sc[:, 0:1], psum[:, 4, 0:1], 1.0 / (KC * U * CHUNK) / HALF_SCALE, None, ALU.mult))
                dve.wait_ge(bank_free, RING + U * (layer + 1))
                for c in range(NCHUNK):
                    y = rows(scratch, c).rearrange("p (r b) -> p r b", b=B)
                    bs = bias_sb[m][:, c * CU * V:(c + 1) * CU * V].unsqueeze(2).to_broadcast([P, CU * V, B])
                    link(dve.scalar_tensor_tensor(y, y, sc[:, 0:1], bs, ALU.mult, ALU.add))
                    n = CU * ROW // 512
                    for q in range(n):
                        last = dve.bn_stats(bst[:, c * n + q, :], scratch[:, (c * n + q) * 512:(c * n + q + 1) * 512])
                        if c == NCHUNK - 1 and q == n - 1:
                            link(last)
                dve.bn_aggr(sc[:, 2:4], bst[:, :, :].rearrange("p n s -> p (n s)")).then_inc(bn_mean_in[m], 1)
                dve.wait_ge(bn_mean_in[m], 1)
                dve.wait_ge(bn_mean[m], 1)
                link(dve.tensor_scalar(sc[:, 6:7], psum[:, 4, 8:9], 1.0 / G, None, ALU.mult))
                link(dve.tensor_tensor(sc[:, 7:8], sc[:, 2:3], sc[:, 6:7], ALU.subtract))
                link(dve.tensor_tensor(sc[:, 8:9], sc[:, 7:8], sc[:, 7:8], ALU.mult))
                dve.tensor_tensor(sc[:, 9:10], sc[:, 8:9], sc[:, 3:4], ALU.add).then_inc(bn_var_in[m], 1)
                dve.wait_ge(bn_var[m], 1)
                link(dve.tensor_scalar(sc[:, 10:11], psum[:, 4, 16:17], 1.0 / G, None, ALU.mult))
                inverse_root(sc[:, 11:12], sc[:, 10:11], sc[:, 15:16], BN_EPS, 2 + 3 * m)
                dve.tensor_tensor(sc[:, 4:5], sc[:, 11:12], gb_sb[:, 2 * m:2 * m + 1], ALU.mult).then_inc(bn_affine[m], 1)
                dve.wait_ge(bn_affine[m], 1)
                link(dve.tensor_tensor(sc[:, 12:13], sc[:, 4:5], sc[:, 6:7], ALU.mult))
                dve.tensor_tensor(sc[:, 5:6], gb_sb[:, 2 * m + 1:2 * m + 2], sc[:, 12:13],
                                  ALU.subtract).then_inc(bn_affine[m], 1)
                for c in range(NCHUNK):
                    dve.wait_ge(relu_made[m], c + 1)
                    link(dve.tensor_scalar(rows(scratch, c), rows(scratch, c), 0.0, None, ALU.is_gt))
                dve.tensor_reduce(sc[:, 13:14], relu_sums[:, :], X, ALU.add).then_inc(relu_red[m], 1)
                dve.wait_ge(relu_total[m], 1)
                link(dve.tensor_scalar(sc[:, 14:15], psum[:, 4, 24:25], 1.0 / (BN_COUNT * C), None, ALU.mult))
                for c in range(NCHUNK):
                    dve.scalar_tensor_tensor(rows(st, c), rows(scratch, c), sc[:, 14:15], rows(st, c),
                                             ALU.mult, ALU.add).then_inc(state_done[layer], 1)

            dve.wait_ge(state_done[2], NCHUNK)
            old = state_b[:, :].rearrange("p (w i b) -> p i b w", w=W, b=B)
            for i in range(V):
                dve.transpose(state_a[:, i * 1024:(i + 1) * 1024].rearrange("p (c b) -> p b c", b=B),
                              old[:, i]).then_inc(transposed, 1)
            dve.wait_ge(transposed, V)
            dve.tensor_reduce(red[:, 0, 0:B], state_a[:, :].rearrange("p (r b) -> p b r", b=B), X,
                              ALU.add).then_inc(gn_red[3], 1)
            dve.wait_ge(squares[3], V)
            dve.tensor_reduce(red[:, 1, 0:B], norm.rearrange("p (r b) -> p b r", b=B), X,
                              ALU.add).then_inc(gn_red[3], 1)
            dve.wait_ge(gn_sums[3], 1)
            mn, rs, ta, tb = (t[:, 0:B] for t in (mean, rstd, tmp_a, tmp_b))
            link(dve.tensor_scalar(mn, psum[:, 4, 0:B], 1.0 / GN_COUNT, None, ALU.mult))
            link(dve.tensor_tensor(ta, mn, mn, ALU.mult))
            link(dve.scalar_tensor_tensor(tb, psum[:, 5, 0:B], 1.0 / GN_COUNT, ta, ALU.mult, ALU.subtract))
            inverse_root(rs, tb, ta, GN_EPS, 6)
            m_op, r_op = (t.unsqueeze(1).to_broadcast([P, C, B]) for t in (mn, rs))
            for i in range(V + 2):
                if i < V:
                    t = xn[i].rearrange("p (c b) -> p c b", b=B)
                    link(dve.tensor_tensor(t, state_a[:, i * 1024:(i + 1) * 1024].rearrange("p (c b) -> p c b", b=B),
                                           m_op, ALU.subtract))
                    dve.tensor_tensor(t, t, r_op, ALU.mult).then_inc(xn_made[3], 1)
                if 1 <= i <= V:
                    dve.wait_ge(xn_made[3], i)
                    dve.wait_ge(t_hi, i)
                    dve.tensor_tensor(xn[i - 1], xn[i - 1], thirds[:, (i - 1) % 2, 0, :], ALU.subtract).then_inc(t_rest, 1)
                if i >= 2:
                    dve.wait_ge(t_rest, i - 1)
                    dve.wait_ge(t_mid, i - 1)
                    dve.tensor_tensor(thirds[:, i % 2, 2, :], xn[i - 2], thirds[:, i % 2, 1, :],
                                      ALU.subtract).then_inc(t_lo, 1)

            def products(k, n):
                for t in range(FT):
                    dve.wait_ge(left_made, k * FT + (t + 1))
                    dve.scalar_tensor_tensor(feats[n][:, t, :], psum[0:FP, 4 + (n * FT + t) % 2, :], linear[:, t:t + 1],
                                             left[:, (n * FT + t) % 2, :], ALU.add, ALU.mult).then_inc(feats_made, 1)

            def add_result(k, n):
                dve.wait_ge(mixed, k + 1)
                res = state_a[:, bass.ds(k * 128, 128)]
                dve.tensor_tensor(res, psum[:, 6 + n, 0:C4 * B], res, ALU.add).then_inc(result_made, 1)

            products(0, 0)
            with dve.Fori(0, NK // 2 - 1) as it:
                products(it * 2 + 1, 1)
                add_result(it * 2, 0)
                products(it * 2 + 2, 0)
                add_result(it * 2 + 1, 1)
            products(NK - 1, 1)
            add_result(NK - 2, 0)
            add_result(NK - 1, 1)

        @block.tensor
        def _(pe):
            pe.wait_ge(consts_in, CONSTS)
            pe.wait_ge(sel_made, 2)
            for layer in range(3):
                st, scratch = states[layer]
                by_v = layer < 2
                pe.wait_ge(gn_red[layer], 2)
                for side in range(2):
                    if by_v:
                        for t in range(2):
                            r = red[:, side, 0:ROW].rearrange("p (q t b) -> p q t b", t=2, b=B)[:, :, t:t + 1, :]
                            last = pe.matmul(psum[:, 4 + side, 0:ROW], in_quadrant,
                                             r.to_broadcast([P, V // 2, 2, B]), start=(t == 0), stop=(t == 1))
                    else:
                        last = pe.matmul(psum[:, 4 + side, :], everywhere, red[:, side, :], start=True, stop=True)
                last.then_inc(gn_sums[layer], 1)

                binary = layer != 1
                cols = 2 * B if binary else B
                with pe.Fori(0, U // RING) as it:
                    for s in range(RING):
                        if s % UC == 0:
                            pe.wait_ge(window_in[s // UC], it * (16 * TAPS * G) + 16 * TAPS * G * (8 * layer + 1))
                        if binary:
                            pe.wait_ge(signs_made, it * RING + (U * (layer // 2) + s + 1))
                            wt = signs[0:KC, s % 2, :]
                        else:
                            pe.wait_ge(w_in[s], it * 16 + 16 * (8 * layer + 1))
                            wt = wring[0:KC, s, :]
                        wt = wt.rearrange("p (v g t o) -> p v g t o", v=V, g=G, t=TAPS)
                        win = window[s // UC].bitcast(F16) if binary else window[s // UC]
                        win = win.rearrange("p (g u s n) -> p g u s n", g=G, u=UC, s=SLOTS)
                        pe.wait_ge(bank_free, it * RING + (U * layer + s + 1))
                        for v in range(V):
                            for t in range(TAPS):
                                for g in range(G):
                                    last = pe.matmul(psum[g * C:(g + 1) * C, s, v * cols:(v + 1) * cols],
                                                     wt[:, v, g, t, :], win[:, g, s % UC, v + t, :],
                                                     start=(v == 0 and t == 0), stop=(v == V - 1 and t == TAPS - 1),
                                                     skip_group_check=True)
                        last.then_inc(conv_done, 1)
                if not binary:
                    continue
                m = layer // 2
                pe.wait_ge(abs_red[m], 1)
                pe.matmul(psum[:, 4, 0:1], everywhere[0:KC, :], abs_sum[0:KC, :], start=True, stop=True).then_inc(abs_total[m], 1)
                pe.wait_ge(bn_mean_in[m], 1)
                pe.matmul(psum[:, 4, 8:9], same_channel, sc[:, 2:3], start=True, stop=True).then_inc(bn_mean[m], 1)
                pe.wait_ge(bn_var_in[m], 1)
                pe.matmul(psum[:, 4, 16:17], same_channel, sc[:, 9:10], start=True, stop=True).then_inc(bn_var[m], 1)
                pe.wait_ge(relu_red[m], 1)
                pe.matmul(psum[:, 4, 24:25], everywhere, sc[:, 13:14], start=True, stop=True).then_inc(relu_total[m], 1)

            pe.wait_ge(gn_red[3], 2)
            for side in range(2):
                last = pe.matmul(psum[:, 4 + side, 0:B], same_pair, red[:, side, 0:B], start=True, stop=True)
            last.then_inc(gn_sums[3], 1)

            def gather(k, n, t):
                cols = parts[:, :, bass.ds(k * (C4 * B), C4 * B)]
                bank = (n * FT + t) % 2
                for side in range(2):
                    last = pe.matmul(psum[0:FP, 2 + 2 * side + bank, :], sel[:, side, t * FP:(t + 1) * FP], cols,
                                     start=True, stop=True)
                last.then_inc(gathered, 1)

            def mix(k, n, slot, t):
                pe.wait_ge(feats_made, k * FT + (t + 1))
                wt = wring[0:FP, slot, 0:W3CHUNK].rearrange("p (t c g o) -> p t c g o", t=FT, c=C4, g=G)
                for c in range(C4):
                    for g in range(G):
                        last = pe.matmul(psum[g * C:(g + 1) * C, 6 + n, c * B:(c + 1) * B], wt[:, t, c, g, :],
                                         feats[n][:, t, (g * C4 + c) * B:(g * C4 + c + 1) * B],
                                         start=(t == 0 and c == 0), stop=(t == FT - 1 and c == C4 - 1),
                                         skip_group_check=True)
                if t == FT - 1:
                    last.then_inc(mixed, 1)

            def step(k, s, fill, ahead=True):
                n = s % 2
                pe.wait_ge(w_in[s], fill)
                for t in range(FT):
                    if ahead:
                        pe.wait_ge(feats_made, k * FT + (FT + t - 1))
                        gather(k + 1, 1 - n, t)
                    mix(k, n, s, t)

            pe.wait_ge(parts_in, 48 * V)
            for t in range(FT):
                if t >= 2:
                    pe.wait_ge(feats_made, t - 1)
                gather(0, 0, t)
            with pe.Fori(0, NK // RING - 1) as it:
                for s in range(RING):
                    step(it * RING + s, s, it * 16 + 16 * (3 * U // RING + 1))
            for s in range(RING):
                k = NK - RING + s
                step(k, s, 16 * (3 * U + NK) // RING, k < NK - 1)


def _rearranged(np, inputs):
    x = inputs["x"]
    xs = x.reshape(B, C, H, G, V).transpose(3, 1, 2, 4, 0).reshape(P, STATE)
    w0 = inputs["L0_conv_weight"].reshape(C, C, H, G, V, TAPS, TAPS)
    w0 = w0.transpose(2, 5, 1, 4, 3, 6, 0).reshape(U, KC, CHUNK)
    w1 = inputs["L1_conv_weights"].reshape(G, V, W, C, C, TAPS, TAPS)
    w1 = w1.transpose(2, 5, 4, 1, 0, 6, 3).reshape(U, KC, CHUNK)
    w2 = inputs["L2_conv_weight"].reshape(C, C, G, V, W, TAPS, TAPS)
    w2 = w2.transpose(4, 6, 1, 3, 2, 5, 0).reshape(U, KC, CHUNK)
    b0 = inputs["L0_conv_bias_p"].reshape(C, H, G, V).transpose(2, 0, 1, 3).reshape(P, U * V)
    b2 = inputs["L2_conv_bias_p"].reshape(C, G, V, W).transpose(1, 0, 3, 2).reshape(P, U * V)
    gb = np.stack([np.tile(inputs[n], G) for n in
                   ("L0_conv_gamma", "L0_conv_beta", "L2_conv_gamma", "L2_conv_beta")], axis=1)
    w3 = inputs["L3_conv_weight"].reshape(C // C4, C4, G, V, FT, FP, W)
    w3 = w3.transpose(3, 0, 5, 4, 1, 2, 6).reshape(NK, FP, W3CHUNK)
    p = np.arange(P)
    mats = np.stack([p[:, None] // C == p // C, np.ones((P, P), bool), p[:, None] % C == p % C,
                     p[:, None] % C // 2 == p % C // 2], axis=1).astype(np.float32)
    own = np.arange(W, dtype=np.int32)
    left = np.concatenate([own, own, inputs["L3_conv_idx_a"].astype(np.int32)])
    right = np.concatenate([own - W, own, inputs["L3_conv_idx_b"].astype(np.int32)])
    index = np.broadcast_to(np.stack([left, right])[None], (KC, 2, FEATS))
    row = (np.arange(KC) % W).astype(np.float32)[:, None]
    lin = (np.arange(FEATS).reshape(FT, FP).T < W).astype(np.float32)
    return {"x": xs, "w0": w0, "w1": w1, "w2": w2, "b0": b0, "b2": b2, "gb": gb, "w3": w3, "mats": mats,
            "row": row, "index": index, "lin": lin}


def kernel(**inputs):
    import numpy as np
    import concourse.bacc as bacc
    from concourse.bass_utils import run_bass_kernel_spmd as run

    arrays = {k: np.ascontiguousarray(v) for k, v in
              _rearranged(np, {k: np.asarray(v) for k, v in inputs.items()}).items()}
    nc = bacc.Bacc("TRN2", target_bir_lowering=False, num_devices=1)
    a = {k: nc.dram_tensor(f"in_{k}", v.shape, mybir.dt.from_np(v.dtype), kind="ExternalInput").ap()
         for k, v in arrays.items()}
    out = nc.dram_tensor("out_0", (P, STATE), F32, kind="ExternalOutput").ap()
    build(nc, a["x"], [a["w0"], a["w1"], a["w2"]], [a["b0"], a["b2"]], a["gb"], a["w3"], a["mats"], a["row"],
          a["index"], a["lin"], out)
    r = run(nc, [{f"in_{k}": v for k, v in arrays.items()}], core_ids=[0])
    got = r.results[0]["out_0"].reshape(G, W, V, C, B)
    return np.ascontiguousarray(got.transpose(4, 3, 0, 2, 1).reshape(B, C, H, W))
```

```python
from contextlib import ExitStack

import concourse.bass as bass
from concourse import mybir

F32 = mybir.dt.float32
F16 = mybir.dt.float16
BF16 = mybir.dt.bfloat16
I32 = mybir.dt.int32
ALU = mybir.AluOpType
ACT = mybir.ActivationFunctionType
X = mybir.AxisListType.X

P = 128
B = C = H = W = 32
G = 4
V = 32 // G
U = 32
ROW = V * B
STATE = U * ROW
TAPS = 3
KC = TAPS * C
KS = 3 * W
CHUNK = V * G * TAPS * C
PAD = U + 2
UC = 2
RING = 4
ACT_ABS = 512
NCHUNK = 8
CU = U // NCHUNK
GN_COUNT = C * H * 2
BN_COUNT = B * H * W
GN_EPS = 1e-5
BN_EPS = 1e-5
HALF_SCALE = 1024.0

PAIRS = W * (W - 1) // 2
FEATS = 2 * W + PAIRS
FT = 5
FP = FEATS // FT
C4 = 4
NK = V * C // C4
PART = RING * C4 * B
NPART = NK // RING
POS = G * C4
FCOL = POS * B
W3CHUNK = FT * POS * W




CENTRE_AFTER, SCALE_AFTER, HIGH_AFTER, LOW_AFTER = 1, 2, 3, 4


SIGNS_AFTER = (5, 7)
MASKS = 2


def build(nc, x, w_conv, bias, gamma_beta, w_mix, mats, sel_rows, sel_index, is_linear, out):
    ctx = ExitStack()
    with ctx:
        def sb(name, shape, dt):
            return ctx.enter_context(nc.sbuf_tensor(name, shape, dt))

        def sem(name):
            return ctx.enter_context(nc.semaphore(name))

        def sems(name, n):
            return [sem(f"{name}{i}") for i in range(n)]

        state_a = sb("state_a", [P, STATE], F32)
        state_b = sb("state_b", [P, STATE], F32)
        work = sb("work", [P, 2 * STATE], F32)
        norm = work[:, 0:STATE]
        norm16 = norm.bitcast(F16)
        WIN = UC * PAD * B
        window = [work[0:KC, STATE + n * WIN:STATE + (n + 1) * WIN] for n in range(2)]
        SPARE = STATE + 2 * WIN
        zeros = work[0:C, SPARE:SPARE + PAD * B]
        sel_i = work[0:KS, SPARE + PAD * B:SPARE + PAD * B + 2 * FEATS].bitcast(I32).rearrange("p (s n) -> p s n", s=2)
        spare = work[0:1, 2 * STATE - 1:2 * STATE]
        wring = sb("wring", [P, RING, CHUNK], F32)
        signs = sb("signs", [P, 2, CHUNK], F16)
        bias_sb = [sb(f"bias{m}", [P, U * V], F32) for m in range(2)]
        gb_sb = sb("gb_sb", [P, 4], F32)
        mats_sb = sb("mats_sb", [P, 4, P], F32)
        in_quadrant, everywhere, same_channel, same_pair = (mats_sb[:, n, :] for n in range(4))
        stats = sb("stats", [P, 6, 512], F32)
        red = stats[:, 0:2, :]
        mean, rstd, tmp_a, tmp_b = (stats[:, n, :] for n in range(2, 6))
        PAIR = ROW // 2
        narrow_rstd = rstd[:, ROW:ROW + PAIR]
        x_half = tmp_b[:, 0:ROW]
        u_sums = stats[:, 0:2, :].rearrange("p s n -> p (s n)")
        u_squares = stats[:, 2:4, :].rearrange("p s n -> p (s n)")
        u_squared = [tmp_a[:, 0:ROW], tmp_b[:, 0:ROW]]
        abs_sums = sb("abs_sums", [P, 2 * U], F32)
        row_sums = sb("row_sums", [P, U * V], F32)
        square_sums = sb("square_sums", [P, U], F32)
        abs_sum = sb("abs_sum", [P, 1], F32)
        sc = sb("sc", [P, 32], F32)
        relu_sums = sb("relu_sums", [P, NCHUNK], F32)
        sel = sb("sel", [KS, 2, FEATS], F16)
        row_id = sb("row_id", [KS, 1], F32)
        linear = sb("linear", [FP, FT], F32)
        parts = work[0:KS, :].bitcast(F16).rearrange("p (g n) -> p g n", g=G)
        feats = [state_b[0:FP, n * FT * FCOL:(n + 1) * FT * FCOL].rearrange("p (t n) -> p t n", t=FT) for n in range(2)]
        BESIDE = 2 * FT * FCOL
        xn = state_b[:, BESIDE:BESIDE + PART]
        hi_lo = signs[:, 0, 0:2 * PART].rearrange("p (k n) -> p k n", k=2)
        left = state_b[0:FP, BESIDE + PART:BESIDE + PART + 2 * FCOL].rearrange("p (s n) -> p s n", s=2)

        psum = ctx.enter_context(nc.psum_tensor("psum", [P, 8, 512], F32))

        image = nc.dram_tensor("image", (C, PAD, PAD, B), I32, kind="Internal").ap()
        parts_dram = nc.dram_tensor("parts_dram", (G, W, 2, NPART, PART), F16, kind="Internal").ap()

        x_in = sems("x_in", NCHUNK)
        consts_in = sem("consts_in")
        mats_in = sem("mats_in")
        zeros_set = sem("zeros_set")
        border_in = sem("border_in")
        sel_made = sem("sel_made")
        w_in = sems("w_in", RING)
        signs_made = sem("signs_made")
        abs_made = sem("abs_made")
        conv_done = sem("conv_done")
        bank_free = sem("bank_free")
        window_in = sems("window_in", 2)
        image_in = [sems(f"image_in{l}_", NCHUNK) for l in range(3)]
        squares = sems("squares", 4)
        gn_red = sems("gn_red", 4)
        gn_acc = sems("gn_acc", 4)
        gn_sums = sems("gn_sums", 4)
        xn_made = sems("xn_made", 4)
        hi_made = sems("hi_made", 3)
        norm_made = sems("norm_made", 3)
        state_done = sems("state_done", 4)
        abs_red = sems("abs_red", 2)
        abs_total = sems("abs_total", 2)
        rows_summed = sem("rows_summed")
        rows_squared = sem("rows_squared")
        u_row_squared = sem("u_row_squared")
        u_row_summed = sem("u_row_summed")
        tile_free = sems("tile_free", 2)
        bn_sums_in = sems("bn_sums_in", 2)
        bn_sums = sems("bn_sums", 2)
        bn_affine = sems("bn_affine", 2)
        relu_made = sems("relu_made", 2)
        masks_made = sems("masks_made", 2)
        masked = sems("masked", 2)
        relu_red = sems("relu_red", 2)
        relu_total = sems("relu_total", 2)
        inverse = sem("inverse")
        root = sem("root")
        dve_chain = sem("dve_chain")
        act_chain = sem("act_chain")
        transposed = sem("transposed")
        centred = sem("centred")
        hi_split = sem("hi_split")
        lo_split = sem("lo_split")
        parts_out = sem("parts_out")
        parts_in = sem("parts_in")
        gathered = sem("gathered")
        left_made = sem("left_made")
        feats_made = sem("feats_made")
        mixed = sem("mixed")
        result_made = sem("result_made")
        out_sem = sem("out_sem")

        block = ctx.enter_context(nc.Block())

        states = [(state_a, state_b), (state_a, state_b), (state_b, state_a)]

        def rows(t, c):
            return t[:, c * CU * ROW:(c + 1) * CU * ROW]

        @block.sync
        def _(sp):
            def load_weights(layer, u, slot):
                if layer < 3:
                    sp.dma_start(wring[0:KC, slot, :], w_conv[layer][u]).then_inc(w_in[slot], 16)
                else:
                    sp.dma_start(wring[0:FP, slot, 0:W3CHUNK], w_mix[u]).then_inc(w_in[slot], 16)

            def load_rows(n, u, taps=range(1, TAPS)):
                for tap in taps:
                    sp.dma_start(window[n][tap * C:(tap + 1) * C, :].bitcast(I32),
                                 image[:, bass.ds(u + tap, UC), :, :].rearrange("c u v b -> c (u v b)")
                                 ).then_inc(window_in[n], 16)

            for c in range(NCHUNK):
                sp.dma_start(rows(state_a, c), rows(x, c)).then_inc(x_in[c], 16)
            sp.dma_start(mats_sb[:, :, :], mats).then_inc(mats_in, 16)
            for s in range(RING):
                load_weights(0, s, s)
            sp.wait_ge(zeros_set, 1)
            zi = zeros.bitcast(I32)
            for edge in (0, PAD - 1):
                sp.dma_start(image[:, edge, :, :].rearrange("c v b -> c (v b)"), zi).then_inc(border_in, 16)
                sp.dma_start(image[:, 1:PAD - 1, edge, :],
                             zi[:, 0:U * B].rearrange("c (u b) -> c u b", u=U)).then_inc(border_in, 16)
            sp.wait_ge(border_in, 64)
            for layer in range(3):
                ni = norm.bitcast(I32).rearrange("p (u n) -> p u n", u=U)
                if layer:
                    for n in range(2):
                        sp.wait_ge(window_in[n], 16 * TAPS * 8 * layer)
                    sp.wait_ge(conv_done, U * layer)
                for c in range(NCHUNK):
                    sp.wait_ge(norm_made[layer], c + 1)
                    for g in range(G):
                        sp.dma_start(image[:, 1 + c * CU:1 + (c + 1) * CU, 1 + g * V:1 + (g + 1) * V, :]
                                     .rearrange("c u v b -> c u (v b)"),
                                     ni[g * C:(g + 1) * C, c * CU:(c + 1) * CU, :]).then_inc(image_in[layer][c], 16)
                    if c < 2:
                        sp.wait_ge(image_in[layer][c], 16 * G)
                        load_rows(c, c * UC, range(c, TAPS))
                for c in range(2, NCHUNK):
                    sp.wait_ge(image_in[layer][c], 16 * G)

                def slot_used(u):
                    if layer == 1:
                        sp.wait_ge(conv_done, U * layer + u + 1)
                    else:
                        sp.wait_ge(signs_made, U * (layer // 2) + u + 1)
                        sp.wait_ge(abs_made, U * (layer // 2) + u + 1)

                with sp.Fori(0, U // RING - 1) as it:
                    for s in range(RING):
                        slot_used(it * RING + s)
                        load_weights(layer, it * RING + s + RING, s)
                        if s % 2:
                            sp.wait_ge(tile_free[s // 2], it + ((U // UC // 2 - 1) * layer + 1))
                            load_rows(s // 2, it * RING + s + 1 + UC)
                for s in range(RING):
                    slot_used(U - RING + s)
                    load_weights(layer + 1, s, s)

            with sp.Fori(0, NPART - 1) as j:
                for s in range(RING):
                    sp.wait_ge(mixed, j * RING + (s + 1))
                    load_weights(3, j * RING + (s + RING), s)

        @block.gpsimd
        def _(pool):
            pool.memset(zeros, 0.0).then_inc(zeros_set, 1)
            for n, (dst, src) in enumerate([(gb_sb[:, :], gamma_beta),
                                            (bias_sb[0][:, :], bias[0]), (bias_sb[1][:, :], bias[1]),
                                            (sel_i, sel_index), (row_id[:, :], sel_rows),
                                            (linear[:, :], is_linear)]):
                pool.dma_start(dst, src).then_inc(consts_in, 16)
            tiles = U // UC // 2

            def copy_rows(n, other_done, reload=True):
                pool.wait_ge(window_in[1 - n], other_done)
                if reload:
                    pool.tensor_tensor(spare, zeros[0:1, 0:1], zeros[0:1, 0:1], ALU.add).then_inc(tile_free[n], 1)
                pool.tensor_copy(window[n][0:C, :], window[1 - n][(TAPS - 1) * C:KC, :]).then_inc(window_in[n], 16)

            for layer in range(3):
                copy_rows(1, 16 * TAPS * (tiles * layer + 1), reload=False)
                with pool.Fori(0, tiles - 1) as it:
                    for n in range(2):
                        pool.wait_ge(conv_done, it * RING + (U * layer + UC * (n + 1)))
                        copy_rows(n, it * (16 * TAPS) + 16 * TAPS * (tiles * layer + 1 + n))

            def one(j):
                return slice(j, j + 1) if isinstance(j, int) else bass.ds(j, 1)

            def store_part(j):
                pool.dma_start(parts_dram[:, :, :, one(j), :].rearrange("g w k o n -> (g w) k (o n)"),
                             hi_lo).then_inc(parts_out, 16)

            def load_part(j):
                for k in range(3):
                    pool.dma_start(parts[k * W:(k + 1) * W, :, bass.ds(j * PART, PART)],
                                 parts_dram[:, :, min(k, 1), one(j), :].rearrange("g w o n -> w g (o n)")
                                 ).then_inc(parts_in, 16)

            pool.wait_ge(lo_split, 1)
            store_part(0)
            pool.wait_ge(parts_out, 16)
            load_part(0)
            with pool.Fori(0, NPART - 1) as j:
                pool.wait_ge(lo_split, j + 2)
                store_part(j + 1)
                pool.wait_ge(parts_out, j * 16 + 32)
                load_part(j + 1)
                pool.wait_ge(result_made, j * RING + RING)
                pool.dma_start(out[:, bass.ds(j * PART, PART)], state_a[:, bass.ds(j * PART, PART)]).then_inc(out_sem, 16)
            last = slice((NPART - 1) * PART, NPART * PART)
            pool.wait_ge(result_made, NK)
            pool.dma_start(out[:, last], state_a[:, last]).then_inc(out_sem, 16)
            pool.wait_ge(out_sem, 16 * NPART)

        CONSTS = 16 * 6

        @block.scalar
        def _(act):
            chain = [0]

            def link(ins):
                chain[0] += 1
                ins.then_inc(act_chain, 1)

            def square(layer):
                st, scratch = states[layer]
                for c in range(NCHUNK):
                    if layer == 0:
                        act.wait_ge(x_in[c], 16)
                    else:
                        act.wait_ge(state_done[0], c + 1)
                    act.activation(rows(scratch, c), rows(st, c), ACT.Square).then_inc(squares[layer], 1)

            def take_root(out, inv, nth):
                act.wait_ge(inverse, nth)
                act.activation(out, inv, ACT.Sqrt).then_inc(root, 1)

            def take_signs(m, u, col, s, unused=tmp_a[0:KC, 0:ACT_ABS]):
                if m or s or not isinstance(u, int):
                    act.wait_ge(signs_made, u + U * m)
                act.activation(unused, wring[0:KC, s, CHUNK - ACT_ABS:CHUNK], ACT.Abs, accum_out=abs_sums[0:KC, col])
                act.activation(signs[0:KC, s % 2, :], wring[0:KC, s, :], ACT.Sign).then_inc(signs_made, 1)

            for layer in range(3):
                st, scratch = states[layer]
                if layer < 2:
                    square(layer)
                if layer != 1:
                    for u in range(2):
                        act.wait_ge(w_in[u], 16 * (8 * layer + 1))
                        if layer:
                            act.wait_ge(conv_done, U * layer)
                        take_signs(layer // 2, u, slice(U + u, U + u + 1), u, row_sums.bitcast(BF16)[0:KC, 0:ACT_ABS])
                if layer < 2:
                    take_root(narrow_rstd, tmp_a[:, 0:PAIR], 2 * layer + 1)
                else:
                    take_root(rstd, tmp_a, 4)
                if layer == 1:
                    def square_u(u, s):
                        act.wait_ge(bank_free, u + (RING + U * layer + 1))
                        act.activation(u_squared[s], scratch[:, bass.ds(u * ROW, ROW)],
                                       ACT.Square).then_inc(u_row_squared, 1)

                    for s in range(2):
                        square_u(s, s)
                    with act.Fori(1, U // 2) as it:
                        for s in range(2):
                            act.wait_ge(u_row_summed, it * 2 + (s - 1))
                            square_u(it * 2 + s, s)
                    continue
                m = layer // 2
                hi = norm16.rearrange("p (u v k b) -> p u v k b", u=U, v=V, k=2)[:, :, :, 0, :]
                t = scratch[:, :].rearrange("p (u v b) -> p u v b", u=U, v=V)
                for c in range(NCHUNK):
                    act.wait_ge(xn_made[layer], c + 1)
                    us = slice(c * CU, (c + 1) * CU)
                    act.activation(hi[:, us], t[:, us], ACT.Copy).then_inc(hi_made[layer], 1)
                    if c in SIGNS_AFTER:
                        u = 2 + SIGNS_AFTER.index(c)
                        act.wait_ge(w_in[u], 16 * (8 * layer + 1))
                        act.wait_ge(conv_done, U * layer + u - 1)
                        take_signs(m, u, slice(U + u, U + u + 1), u)
                def square_row(u, col):
                    if m or not isinstance(u, int) or u:
                        act.wait_ge(rows_squared, u + U * m)
                    act.wait_ge(bank_free, u + (RING + U * layer + 1))
                    act.activation(tmp_b[:, 0:ROW], scratch[:, bass.ds(u * ROW, ROW)], ACT.Square,
                                   accum_out=square_sums[:, col]).then_inc(rows_squared, 1)

                for u in range(RING - 2):
                    square_row(u, slice(u, u + 1))
                with act.Fori(1, U // RING) as it:
                    for s in range(RING):
                        act.wait_ge(w_in[s], it * 16 + 16 * (8 * layer + 1))
                        act.wait_ge(conv_done, it * RING + (U * layer + s - 1))
                        take_signs(m, it * RING + s, bass.ds(it * RING + (U + s), 1), s)
                        square_row(it * RING + (s - 2), bass.ds(it * RING + (s - 2), 1))
                for u in range(U - 2, U):
                    square_row(u, slice(u, u + 1))
                take_root(sc[:, 11:12], sc[:, 15:16], 2 + 3 * m)
                for c in range(NCHUNK):
                    act.wait_ge(bn_affine[m], c + 1)
                    act.activation(rows(scratch, c), rows(scratch, c), ACT.Relu,
                                   accum_out=relu_sums[:, c:c + 1]).then_inc(relu_made[m], 1)
                for c in range(MASKS, NCHUNK):
                    act.wait_ge(relu_made[m], c + 1)
                    act.activation(rows(scratch, c), rows(scratch, c), ACT.Sign).then_inc(masks_made[m], 1)

            for i in range(V):
                act.wait_ge(transposed, i + 1)
                act.activation(norm[:, i * 1024:(i + 1) * 1024], state_a[:, i * 1024:(i + 1) * 1024],
                               ACT.Square).then_inc(squares[3], 1)
            take_root(rstd[:, 0:B], tmp_a[:, 0:B], 6)

            def high(j):
                act.wait_ge(xn_made[3], j + 1)
                act.activation(hi_lo[:, 0, :], xn, ACT.Copy).then_inc(hi_split, 1)

            def copy_left(k, parity, t):
                act.wait_ge(gathered, k * FT + (t + 1))
                n = (parity * FT + t) % 2
                act.activation(left[:, n, :], psum[0:FP, 2 + n, :], ACT.Copy,
                               scale=1.0 / HALF_SCALE / HALF_SCALE).then_inc(left_made, 1)

            high(0)
            for t in range(FT):
                copy_left(0, 0, t)
            with act.Fori(0, NPART - 1) as j:
                for s in range(RING):
                    for t in range(FT):
                        copy_left(j * RING + (s + 1), (s + 1) % 2, t)
                        if s == 0 and t == HIGH_AFTER:
                            act.wait_ge(parts_out, j * 16 + 16)
                            high(j + 1)
            for k in range(NK - RING + 1, NK):
                for t in range(FT):
                    copy_left(k, k % 2, t)

        @block.vector
        def _(dve):
            chain = [0]

            def link(ins):
                chain[0] += 1
                ins.then_inc(dve_chain, 1)
                dve.wait_ge(dve_chain, chain[0])

            def inverse_root(out, var, tmp, eps, nth):
                link(dve.tensor_scalar(var, var, eps, None, ALU.add))
                dve.reciprocal(tmp, var).then_inc(inverse, 1)
                dve.wait_ge(root, nth)
                link(dve.tensor_tensor(tmp, out, out, ALU.mult))
                link(dve.tensor_tensor(tmp, tmp, var, ALU.mult))
                link(dve.tensor_scalar(tmp, tmp, -0.5, 1.5, ALU.mult, ALU.add))
                link(dve.tensor_tensor(out, out, tmp, ALU.mult))

            dve.memset(sc[:, :], 0.0).then_inc(bank_free, RING)
            def pairs_of_v(t):
                return t.rearrange("p (u r) -> p r u", r=ROW)

            def pairs_of_u(t):
                return t.rearrange("p (u k b) -> p u b k", u=U // 2, b=B)

            for layer in range(3):
                st, scratch = states[layer]
                by_v = layer < 2
                if by_v:
                    half = U // 2 * ROW
                    if layer == 0:
                        for c in range(NCHUNK // 2):
                            dve.wait_ge(x_in[c], 16)
                        dve.tensor_reduce(x_half, pairs_of_v(st[:, 0:half]), X, ALU.add).then_inc(gn_red[0], 1)
                    for h in range(2):
                        dve.wait_ge(squares[layer], NCHUNK // 2 * (h + 1))
                        dve.tensor_reduce(red[:, 1, h * ROW:(h + 1) * ROW],
                                          pairs_of_v(scratch[:, h * half:(h + 1) * half]), X, ALU.add
                                          ).then_inc(gn_red[layer], 1)
                    dve.wait_ge(gn_acc[layer], 1)
                    dve.tensor_copy(red[:, 0, 0:ROW], psum[:, 4, 0:ROW]).then_inc(gn_red[layer], 1)
                dve.wait_ge(gn_sums[layer], 1)
                if by_v:
                    def each(t):
                        return t[:, 0:PAIR].rearrange("p (q b) -> p q b", b=B)

                    def both(t):
                        return t[:, 0:ROW].rearrange("p (q t b) -> p q t b", t=2, b=B)

                    sums, sums2, ta, tb, rs = (each(t) for t in (psum[:, 5, :], psum[:, 6, :], tmp_a, tmp_b, narrow_rstd))
                    link(dve.tensor_scalar(both(mean), sums.unsqueeze(2).to_broadcast([P, V // 2, 2, B]),
                                           1.0 / GN_COUNT / C, None, ALU.mult))
                    mn = both(mean)[:, :, 0, :]
                else:
                    sums, sums2, mn, ta, tb, rs = psum[:, 5, :], psum[:, 6, :], mean, tmp_a, tmp_b, rstd
                    link(dve.tensor_scalar(mn, sums, 1.0 / GN_COUNT, None, ALU.mult))
                link(dve.tensor_tensor(ta, mn, mn, ALU.mult))
                link(dve.scalar_tensor_tensor(tb, sums2, 1.0 / GN_COUNT, ta, ALU.mult, ALU.subtract))
                inverse_root(rs, tb, ta, GN_EPS, 2 * layer + 1 - layer // 2)
                if by_v:
                    link(dve.tensor_scalar(both(rstd), rs.unsqueeze(2).to_broadcast([P, V // 2, 2, B]),
                                           1.0 if layer else HALF_SCALE, None, ALU.mult))
                else:
                    link(dve.tensor_scalar(rs, rs, HALF_SCALE, None, ALU.mult))
                mn, rs = (t[:, 0:ROW] if by_v else t for t in (mean, rstd))
                dst = norm if layer == 1 else scratch
                halves = norm16.rearrange("p (u v k b) -> p u v k b", u=U, v=V, k=2)
                t4 = scratch[:, :].rearrange("p (u v b) -> p u v b", u=U, v=V)
                for c in range(NCHUNK + 1):
                    if c < NCHUNK:
                        if by_v:
                            view = [rows(t, c).rearrange("p (u r) -> p u r", r=ROW) for t in (st, dst)]
                            m_op, r_op = (t.unsqueeze(1).to_broadcast([P, CU, ROW]) for t in (mn, rs))
                        else:
                            view = [rows(t, c).rearrange("p (u k b) -> p u k b", u=CU // 2, b=B) for t in (st, dst)]
                            m_op, r_op = (t[:, c * CU // 2 * B:(c + 1) * CU // 2 * B]
                                          .rearrange("p (u b) -> p u b", b=B)
                                          .unsqueeze(2).to_broadcast([P, CU // 2, 2 * V, B]) for t in (mn, rs))
                        link(dve.tensor_tensor(view[1], view[0], m_op, ALU.subtract))
                        dve.tensor_tensor(view[1], view[1], r_op, ALU.mult).then_inc(
                            norm_made[1] if layer == 1 else xn_made[layer], 1)
                    if c and layer != 1:
                        us = slice((c - 1) * CU, c * CU)
                        dve.wait_ge(xn_made[layer], c)
                        dve.wait_ge(hi_made[layer], c)
                        dve.tensor_tensor(halves[:, us, :, 1, :], t4[:, us], halves[:, us, :, 0, :],
                                          ALU.subtract).then_inc(norm_made[layer], 1)

                if layer == 0:
                    dve.wait_ge(consts_in, CONSTS)
                    for side in range(2):
                        dve.tensor_scalar(sel[:, side, :], sel_i[:, side, :], row_id[:, 0:1], None,
                                          ALU.is_equal).then_inc(sel_made, 1)

                if layer == 1:
                    src = st[:, :].rearrange("p (h v b) -> p h v b", h=H, b=B)
                    for wg in range(G):
                        with dve.Fori(0, V // RING) as half:
                            for s in range(RING):
                                dve.wait_ge(conv_done, half * RING + (U * layer + wg * V + s + 1))
                                for g in range(G):
                                    res = scratch[g * C:(g + 1) * C, bass.ds((half * RING + (wg * V + s)) * ROW, ROW)]
                                    old = src[wg * C:(wg + 1) * C, g * V:(g + 1) * V, bass.ds(half * RING + s, 1), :]
                                    last = dve.tensor_tensor(
                                        res.rearrange("p (v b) -> p v b", b=B),
                                        psum[g * C:(g + 1) * C, s % 2 * 2:s % 2 * 2 + 2, :].rearrange(
                                            "p k (v g b) -> p (k v) g b", g=G, b=B)[:, :, g, :],
                                        old.rearrange("p v o b -> p v (o b)"), ALU.add)
                                last.then_inc(bank_free, 1)
                                u = half * RING + (wg * V + s)
                                res = scratch[:, bass.ds(u * ROW, ROW)].rearrange("p (v b) -> p b v", b=B)
                                dve.wait_ge(bank_free, half * RING + (RING + U * layer + wg * V + s + 1))
                                dve.tensor_reduce(u_sums[:, bass.ds(u * B, B)], res, X, ALU.add)
                                dve.wait_ge(u_row_squared, half * RING + (wg * V + s + 1))
                                dve.tensor_reduce(u_squares[:, bass.ds(u * B, B)],
                                                  u_squared[s % 2].rearrange("p (v b) -> p b v", b=B),
                                                  X, ALU.add).then_inc(u_row_summed, 1)
                    continue

                m = layer // 2
                bias_sq = tmp_b[:, ROW:2 * ROW]
                dve.wait_ge(consts_in, CONSTS)
                link(dve.tensor_tensor(bias_sq, bias_sb[m][:, :], bias_sb[m][:, :], ALU.mult))
                link(dve.tensor_reduce(sc[:, 16:17], bias_sb[m][:, :], X, ALU.add))
                link(dve.tensor_reduce(sc[:, 17:18], bias_sq, X, ALU.add))
                with dve.Fori(0, U // RING) as it:
                    for s in range(RING):
                        u = it * RING + s
                        dve.wait_ge(w_in[s], it * 16 + 16 * (8 * layer + 1))
                        dve.tensor_reduce(abs_sums[0:KC, bass.ds(u, 1)], wring[0:KC, s, 0:CHUNK - ACT_ABS], X, ALU.add,
                                          apply_absolute_value=True).then_inc(abs_made, 1)
                        dve.wait_ge(conv_done, it * RING + (U * layer + s + 1))
                        dve.tensor_reduce(
                            scratch[:, bass.ds(u * ROW, ROW)].rearrange("p (v b) -> p v b", b=B),
                            psum[:, s, :].rearrange("p (v k b) -> p v b k", k=2, b=B), X, ALU.add
                        ).then_inc(bank_free, 1)
                        dve.wait_ge(bank_free, it * RING + (RING + U * layer + s + 1))
                        dve.tensor_reduce(row_sums[:, bass.ds(u * V, V)],
                                          scratch[:, bass.ds(u * ROW, ROW)].rearrange("p (v b) -> p v b", b=B),
                                          X, ALU.add).then_inc(rows_summed, 1)
                dve.wait_ge(abs_made, U * (m + 1))
                dve.wait_ge(signs_made, U * (m + 1))
                dve.tensor_reduce(abs_sum[0:KC, :], abs_sums[0:KC, :], X, ALU.add).then_inc(abs_red[m], 1)
                dve.wait_ge(rows_summed, U * (m + 1))
                link(dve.tensor_tensor(bias_sq, row_sums[:, :], bias_sb[m][:, :], ALU.mult))
                link(dve.tensor_reduce(sc[:, 18:19], bias_sq, X, ALU.add))
                link(dve.tensor_reduce(sc[:, 19:20], row_sums[:, :], X, ALU.add))
                dve.wait_ge(rows_squared, U * (m + 1))
                link(dve.tensor_reduce(sc[:, 20:21], square_sums[:, :], X, ALU.add))
                link(dve.tensor_scalar(sc[:, 21:22], sc[:, 18:19], 2.0, None, ALU.mult))
                link(dve.tensor_scalar(sc[:, 22:24], sc[:, 16:18], float(B), None, ALU.mult))
                dve.wait_ge(abs_total[m], 1)
                link(dve.tensor_scalar(sc[:, 0:1], psum[:, 4, 0:1], 1.0 / (KC * U * CHUNK) / HALF_SCALE, None, ALU.mult))
                link(dve.scalar_tensor_tensor(sc[:, 2:3], sc[:, 19:20], sc[:, 0:1], sc[:, 22:23], ALU.mult, ALU.add))
                link(dve.scalar_tensor_tensor(sc[:, 24:25], sc[:, 20:21], sc[:, 0:1], sc[:, 21:22], ALU.mult, ALU.add))
                dve.scalar_tensor_tensor(sc[:, 3:4], sc[:, 24:25], sc[:, 0:1], sc[:, 23:24], ALU.mult,
                                         ALU.add).then_inc(bn_sums_in[m], 1)
                dve.wait_ge(bn_sums[m], 1)
                link(dve.tensor_scalar(sc[:, 6:8], psum[:, 4, 8:10], 1.0 / BN_COUNT, None, ALU.mult))
                link(dve.tensor_tensor(sc[:, 8:9], sc[:, 6:7], sc[:, 6:7], ALU.mult))
                link(dve.tensor_tensor(sc[:, 10:11], sc[:, 7:8], sc[:, 8:9], ALU.subtract))
                inverse_root(sc[:, 11:12], sc[:, 10:11], sc[:, 15:16], BN_EPS, 2 + 3 * m)
                link(dve.tensor_tensor(sc[:, 4:5], sc[:, 11:12], gb_sb[:, 2 * m:2 * m + 1], ALU.mult))
                link(dve.tensor_tensor(sc[:, 12:13], sc[:, 4:5], sc[:, 6:7], ALU.mult))
                link(dve.tensor_tensor(sc[:, 5:6], gb_sb[:, 2 * m + 1:2 * m + 2], sc[:, 12:13], ALU.subtract))
                link(dve.tensor_tensor(sc[:, 25:26], sc[:, 4:5], sc[:, 0:1], ALU.mult))
                offset = tmp_b[:, 0:ROW]
                link(dve.tensor_scalar(offset, bias_sb[m][:, :], sc[:, 4:5], sc[:, 5:6], ALU.mult, ALU.add))
                for c in range(NCHUNK):
                    y = rows(scratch, c).rearrange("p (r b) -> p r b", b=B)
                    off = offset[:, c * CU * V:(c + 1) * CU * V].unsqueeze(2).to_broadcast([P, CU * V, B])
                    dve.scalar_tensor_tensor(y, y, sc[:, 25:26], off, ALU.mult, ALU.add).then_inc(bn_affine[m], 1)
                for c in range(MASKS):
                    dve.wait_ge(relu_made[m], c + 1)
                    dve.tensor_scalar(rows(scratch, c), rows(scratch, c), 0.0, None, ALU.is_gt).then_inc(masked[m], 1)
                dve.wait_ge(relu_made[m], NCHUNK)
                dve.tensor_reduce(sc[:, 13:14], relu_sums[:, :], X, ALU.add).then_inc(relu_red[m], 1)
                dve.wait_ge(relu_total[m], 1)
                link(dve.tensor_scalar(sc[:, 14:15], psum[:, 4, 24:25], 1.0 / (BN_COUNT * C), None, ALU.mult))
                for c in range(NCHUNK):
                    if c < MASKS:
                        dve.wait_ge(masked[m], c + 1)
                    else:
                        dve.wait_ge(masks_made[m], c - MASKS + 1)
                    dve.scalar_tensor_tensor(rows(st, c), rows(scratch, c), sc[:, 14:15], rows(st, c),
                                             ALU.mult, ALU.add).then_inc(state_done[layer], 1)

            dve.wait_ge(state_done[2], NCHUNK)
            old = state_b[:, :].rearrange("p (w i b) -> p i b w", w=W, b=B)
            for i in range(V):
                dve.transpose(state_a[:, i * 1024:(i + 1) * 1024].rearrange("p (c b) -> p b c", b=B),
                              old[:, i]).then_inc(transposed, 1)
            dve.wait_ge(transposed, V)
            dve.wait_ge(squares[3], V)
            dve.tensor_reduce(red[:, 1, 0:B], norm.rearrange("p (r b) -> p b r", b=B), X,
                              ALU.add).then_inc(gn_red[3], 1)
            dve.wait_ge(gn_acc[3], 1)
            link(dve.tensor_reduce(red[:, 0, 0:B], psum[:, 4, :].rearrange("p (c b) -> p b c", b=B), X, ALU.add))
            dve.wait_ge(gn_sums[3], 1)
            mn, rs, ta, tb = (t[:, 0:B] for t in (mean, rstd, tmp_a, tmp_b))
            link(dve.tensor_scalar(mn, red[:, 0, 0:B], 1.0 / GN_COUNT, None, ALU.mult))
            link(dve.tensor_tensor(ta, mn, mn, ALU.mult))
            link(dve.scalar_tensor_tensor(tb, psum[:, 5, 0:B], 1.0 / GN_COUNT, ta, ALU.mult, ALU.subtract))
            inverse_root(rs, tb, ta, GN_EPS, 6)
            link(dve.tensor_scalar(rs, rs, HALF_SCALE, None, ALU.mult))
            m_op, r_op = (t.unsqueeze(1).to_broadcast([P, PART // B, B]) for t in (mn, rs))

            def centre(j):
                dve.tensor_tensor(xn.rearrange("p (c b) -> p c b", b=B),
                                  state_a[:, bass.ds(j * PART, PART)].rearrange("p (c b) -> p c b", b=B),
                                  m_op, ALU.subtract).then_inc(centred, 1)

            def scale(j):
                dve.wait_ge(centred, j + 1)
                t = xn.rearrange("p (c b) -> p c b", b=B)
                dve.tensor_tensor(t, t, r_op, ALU.mult).then_inc(xn_made[3], 1)

            def low(j):
                dve.wait_ge(xn_made[3], j + 1)
                dve.wait_ge(hi_split, j + 1)
                dve.tensor_tensor(hi_lo[:, 1, :], xn, hi_lo[:, 0, :], ALU.subtract).then_inc(lo_split, 1)

            centre(0)
            scale(0)
            low(0)

            def product(k, n, t):
                dve.wait_ge(left_made, k * FT + (t + 1))
                dve.scalar_tensor_tensor(feats[n][:, t, :], psum[0:FP, 4 + (n * FT + t) % 2, :], linear[:, t:t + 1],
                                         left[:, (n * FT + t) % 2, :], ALU.add, ALU.mult).then_inc(feats_made, 1)

            def add_result(k, n):
                dve.wait_ge(mixed, k + 1)
                res = state_a[:, bass.ds(k * 128, 128)]
                for g in range(G):
                    q = slice(g * C, (g + 1) * C)
                    out_g = res[q, :].rearrange("p (c b) -> p c b", b=B)
                    last = dve.tensor_tensor(
                        out_g, psum[q, 6 + n, :].rearrange("p (c g b) -> p c g b", g=G, b=B)[:, :, g, :], out_g, ALU.add)
                last.then_inc(result_made, 1)

            for t in range(FT):
                product(0, 0, t)
            product(1, 1, 0)
            with dve.Fori(0, NPART - 1) as j:
                for s in range(RING):
                    for t in range(1, FT):
                        product(j * RING + (s + 1), (s + 1) % 2, t)
                        for step, after in ((centre, CENTRE_AFTER), (scale, SCALE_AFTER), (low, LOW_AFTER)):
                            if s == 0 and t == after:
                                step(j + 1)
                    product(j * RING + (s + 2), s % 2, 0)
                    add_result(j * RING + s, s % 2)
            for s in range(RING):
                k = NK - RING + s
                if k + 1 < NK:
                    for t in range(1, FT):
                        product(k + 1, (s + 1) % 2, t)
                if k + 2 < NK:
                    product(k + 2, s % 2, 0)
                add_result(k, s % 2)

        @block.tensor
        def _(pe):
            pe.wait_ge(mats_in, 16)
            for layer in range(3):
                st, scratch = states[layer]
                by_v = layer < 2
                if by_v:
                    first = 0 if layer else U // 2
                    for u in range(first, U):
                        if u % CU == 0:
                            if layer:
                                pe.wait_ge(state_done[0], u // CU + 1)
                            else:
                                pe.wait_ge(x_in[u // CU], 16)
                        last = pe.matmul(psum[:, 4, 0:ROW], in_quadrant, st[:, u * ROW:(u + 1) * ROW],
                                         start=(u == first), stop=(layer == 1 and u == U - 1))
                    if layer == 0:
                        pe.wait_ge(gn_red[0], 1)
                        last = pe.matmul(psum[:, 4, 0:ROW], in_quadrant, x_half, start=False, stop=True)
                    last.then_inc(gn_acc[layer], 1)
                    pe.wait_ge(gn_red[layer], 4 if layer == 0 else 3)
                    for side in range(2):
                        views = [red[:, side, h * ROW:(h + 1) * ROW].rearrange("p (q t b) -> p q t b", t=2, b=B)[:, :, t, :]
                                 for h in range(side + 1) for t in range(2)]
                        for n, r in enumerate(views):
                            last = pe.matmul(psum[:, 5 + side, 0:PAIR], in_quadrant, r,
                                             start=(n == 0), stop=(n == len(views) - 1))
                else:
                    early = U // 2 - 2
                    for pairs, need in ((slice(0, early), 2 * early), (slice(early, U // 2), U)):
                        pe.wait_ge(u_row_summed, need)
                        for side in range(2):
                            for t in range(2):
                                r = (u_sums, u_squares)[side].rearrange("p (u t b) -> p u t b", t=2, b=B)[:, pairs, t, :]
                                last = pe.matmul(psum[:, 5 + side, pairs.start * B:pairs.stop * B], everywhere, r,
                                                 start=(t == 0), stop=(t == 1))
                last.then_inc(gn_sums[layer], 1)

                binary = layer != 1
                cols = 2 * B if binary else B
                with pe.Fori(0, U // RING) as it:
                    for s in range(RING):
                        if s % UC == 0:
                            pe.wait_ge(window_in[s // UC], it * (16 * TAPS) + 16 * TAPS * (8 * layer + 1))
                        if binary:
                            pe.wait_ge(signs_made, it * RING + (U * (layer // 2) + s + 1))
                            wt = signs[0:KC, s % 2, :]
                        else:
                            pe.wait_ge(w_in[s], it * 16 + 16 * (8 * layer + 1))
                            wt = wring[0:KC, s, :]
                        win = window[s // UC].bitcast(F16) if binary else window[s // UC]
                        win = win.rearrange("p (u v n) -> p u v n", u=UC, v=PAD)[:, s % UC, :, :]
                        if binary:
                            wt = wt.rearrange("p (v g t o) -> p v g t o", v=V, g=G, t=TAPS)
                            pe.wait_ge(bank_free, it * RING + (U * layer + s + 1))
                            for v in range(V):
                                for t in range(TAPS):
                                    for g in range(G):
                                        last = pe.matmul(psum[g * C:(g + 1) * C, s, v * cols:(v + 1) * cols],
                                                         wt[:, v, g, t, :], win[:, g * V + v + t, :],
                                                         start=(v == 0 and t == 0), stop=(v == V - 1 and t == TAPS - 1),
                                                         skip_group_check=True)
                        else:
                            wt = wt.rearrange("p (v t m) -> p v t m", v=V, t=TAPS)
                            pe.wait_ge(bank_free, it * RING + (RING + U * layer + s - 1))
                            for v in range(V):
                                for t in range(TAPS):
                                    bank = s % 2 * 2 + v // (V // 2)
                                    col = v % (V // 2) * G * cols
                                    last = pe.matmul(psum[:, bank, col:col + G * cols], wt[:, v, t, :],
                                                     win[:, v + t:v + t + (G - 1) * V + 1:V, :],
                                                     start=(v % (V // 2) == 0 and t == 0),
                                                     stop=(v % (V // 2) == V // 2 - 1 and t == TAPS - 1),
                                                     skip_group_check=True)
                        last.then_inc(conv_done, 1)
                if not binary:
                    continue
                m = layer // 2
                pe.wait_ge(abs_red[m], 1)
                pe.matmul(psum[:, 4, 0:1], everywhere[0:KC, :], abs_sum[0:KC, :], start=True, stop=True).then_inc(abs_total[m], 1)
                pe.wait_ge(bn_sums_in[m], 1)
                pe.matmul(psum[:, 4, 8:10], same_channel, sc[:, 2:4], start=True, stop=True).then_inc(bn_sums[m], 1)
                pe.wait_ge(relu_red[m], 1)
                pe.matmul(psum[:, 4, 24:25], everywhere, sc[:, 13:14], start=True, stop=True).then_inc(relu_total[m], 1)

            for i in range(V):
                pe.wait_ge(transposed, i + 1)
                for h in range(2):
                    last = pe.matmul(psum[:, 4, :], same_pair, state_a[:, (2 * i + h) * 512:(2 * i + h + 1) * 512],
                                     start=(i == 0 and h == 0), stop=(i == V - 1 and h == 1))
            last.then_inc(gn_acc[3], 1)
            pe.wait_ge(gn_red[3], 1)
            pe.matmul(psum[:, 5, 0:B], same_pair, red[:, 1, 0:B], start=True, stop=True).then_inc(gn_sums[3], 1)
            pe.wait_ge(sel_made, 2)

            def gather(k, n, t):
                cols = parts[:, :, bass.ds(k * (C4 * B), C4 * B)]
                bank = (n * FT + t) % 2
                for side in range(2):
                    last = pe.matmul(psum[0:FP, 2 + 2 * side + bank, :], sel[:, side, t * FP:(t + 1) * FP], cols,
                                     start=True, stop=True)
                last.then_inc(gathered, 1)

            def mix(k, n, slot, t):
                pe.wait_ge(feats_made, k * FT + (t + 1))
                wt = wring[0:FP, slot, 0:W3CHUNK].rearrange("p (t c m) -> p t c m", t=FT, c=C4)
                f = feats[n][:, t, :].rearrange("p (g c b) -> p c g b", g=G, c=C4)
                for c in range(C4):
                    last = pe.matmul(psum[:, 6 + n, c * G * B:(c + 1) * G * B], wt[:, t, c, :], f[:, c, :, :],
                                     start=(t == 0 and c == 0), stop=(t == FT - 1 and c == C4 - 1),
                                     skip_group_check=True)
                if t == FT - 1:
                    last.then_inc(mixed, 1)

            def step(k, s, fill, ahead=True):
                n = s % 2
                pe.wait_ge(w_in[s], fill)
                for t in range(FT):
                    if ahead:
                        pe.wait_ge(feats_made, k * FT + (FT + t - 1))
                        gather(k + 1, 1 - n, t)
                    mix(k, n, s, t)

            pe.wait_ge(parts_in, 48)
            for t in range(FT):
                if t >= 2:
                    pe.wait_ge(feats_made, t - 1)
                gather(0, 0, t)
            with pe.Fori(0, NPART - 1) as j:
                for s in range(RING):
                    if s == RING - 1:
                        pe.wait_ge(parts_in, j * 48 + 96)
                    step(j * RING + s, s, j * 16 + 16 * (3 * U // RING + 1))
            for s in range(RING):
                k = NK - RING + s
                step(k, s, 16 * (3 * U + NK) // RING, k < NK - 1)


def _rearranged(np, inputs):
    x = inputs["x"]
    xs = x.reshape(B, C, H, G, V).transpose(3, 1, 2, 4, 0).reshape(P, STATE)
    w0 = inputs["L0_conv_weight"].reshape(C, C, H, G, V, TAPS, TAPS)
    w0 = w0.transpose(2, 5, 1, 4, 3, 6, 0).reshape(U, KC, CHUNK)
    w1 = inputs["L1_conv_weights"].reshape(G, V, W, C, C, TAPS, TAPS)
    w1 = w1.transpose(2, 5, 4, 1, 6, 0, 3).reshape(U, KC, CHUNK)
    w2 = inputs["L2_conv_weight"].reshape(C, C, G, V, W, TAPS, TAPS)
    w2 = w2.transpose(4, 6, 1, 3, 2, 5, 0).reshape(U, KC, CHUNK)
    b0 = inputs["L0_conv_bias_p"].reshape(C, H, G, V).transpose(2, 0, 1, 3).reshape(P, U * V)
    b2 = inputs["L2_conv_bias_p"].reshape(C, G, V, W).transpose(1, 0, 3, 2).reshape(P, U * V)
    gb = np.stack([np.tile(inputs[n], G) for n in
                   ("L0_conv_gamma", "L0_conv_beta", "L2_conv_gamma", "L2_conv_beta")], axis=1)
    w3 = inputs["L3_conv_weight"].reshape(C // C4, C4, G, V, FT, FP, W)
    w3 = w3.transpose(3, 0, 5, 4, 1, 2, 6).reshape(NK, FP, W3CHUNK)
    p = np.arange(P)
    mats = np.stack([p[:, None] // C == p // C, np.ones((P, P), bool), p[:, None] % C == p % C,
                     p[:, None] % C // 2 == p % C // 2], axis=1).astype(np.float32)
    own = np.arange(W, dtype=np.int32)
    left = np.concatenate([own, own, inputs["L3_conv_idx_a"].astype(np.int32)])
    right = np.concatenate([own - W, own, inputs["L3_conv_idx_b"].astype(np.int32)])
    index = np.broadcast_to(np.stack([left, right])[None], (KS, 2, FEATS))
    row = np.where(np.arange(KS) < 2 * W, np.arange(KS) % W, 2 * W).astype(np.float32)[:, None]
    lin = (np.arange(FEATS).reshape(FT, FP).T < W).astype(np.float32) * np.float32(HALF_SCALE)
    return {"x": xs, "w0": w0, "w1": w1, "w2": w2, "b0": b0, "b2": b2, "gb": gb, "w3": w3, "mats": mats,
            "row": row, "index": index, "lin": lin}


def kernel(**inputs):
    import numpy as np
    import concourse.bacc as bacc
    from concourse.bass_utils import run_bass_kernel_spmd as run

    arrays = {k: np.ascontiguousarray(v) for k, v in
              _rearranged(np, {k: np.asarray(v) for k, v in inputs.items()}).items()}
    nc = bacc.Bacc("TRN2", target_bir_lowering=False, num_devices=1)
    a = {k: nc.dram_tensor(f"in_{k}", v.shape, mybir.dt.from_np(v.dtype), kind="ExternalInput").ap()
         for k, v in arrays.items()}
    out = nc.dram_tensor("out_0", (P, STATE), F32, kind="ExternalOutput").ap()
    build(nc, a["x"], [a["w0"], a["w1"], a["w2"]], [a["b0"], a["b2"]], a["gb"], a["w3"], a["mats"], a["row"],
          a["index"], a["lin"], out)
    r = run(nc, [{f"in_{k}": v for k, v in arrays.items()}], core_ids=[0])
    got = r.results[0]["out_0"].reshape(G, W, V, C, B)
    return np.ascontiguousarray(got.transpose(4, 3, 0, 2, 1).reshape(B, C, H, W))
```

```python
from contextlib import ExitStack

import concourse.bass as bass
from concourse import mybir

F32 = mybir.dt.float32
F16 = mybir.dt.float16
BF16 = mybir.dt.bfloat16
I32 = mybir.dt.int32
ALU = mybir.AluOpType
ACT = mybir.ActivationFunctionType
X = mybir.AxisListType.X

P = 128
B = C = H = W = 32
G = 4
V = 32 // G
U = 32
ROW = V * B
STATE = U * ROW
TAPS = 3
KC = TAPS * C
KS = 3 * W
CHUNK = V * G * TAPS * C
PAD = U + 2
UC = 2
RING = 4
ACT_ABS = 640
NCHUNK = 8
CU = U // NCHUNK
GN_COUNT = C * H * 2
BN_COUNT = B * H * W
GN_EPS = 1e-5
BN_EPS = 1e-5
HALF_SCALE = 1024.0

PAIRS = W * (W - 1) // 2
FEATS = 2 * W + PAIRS
PT = 4
FT = 1 + PT
FP = PAIRS // PT
ROWS = [2 * W] + PT * [FP]
COLS = [sum(ROWS[:t]) for t in range(FT)]
C4 = 4
NK = V * C // C4
PART = RING * C4 * B
NPART = NK // RING
POS = G * C4
FCOL = POS * B
W3CHUNK = FT * POS * W

CENTRE_AFTER, SCALE_AFTER, HIGH_AFTER, LOW_AFTER = 1, 2, 3, 4

SIGNS_AFTER = (5, 7)
WEIGHTS_AFTER = (1, 6, 7)
ROWS_AFTER = 5
X_PIECES = 5
MASKS = 2


def build(nc, x, w_conv, bias, gamma_beta, w_own, w_pairs, mats, sel_rows, sel_index, own_affine, out):
    ctx = ExitStack()
    with ctx:
        def sb(name, shape, dt):
            return ctx.enter_context(nc.sbuf_tensor(name, shape, dt))

        def sem(name):
            return ctx.enter_context(nc.semaphore(name))

        def sems(name, n):
            return [sem(f"{name}{i}") for i in range(n)]

        state_a = sb("state_a", [P, STATE], F32)
        state_b = sb("state_b", [P, STATE], F32)
        work = sb("work", [P, 2 * STATE], F32)
        norm = work[:, 0:STATE]
        norm16 = norm.bitcast(F16)
        WIN = UC * PAD * B
        window = [work[0:KC, STATE + n * WIN:STATE + (n + 1) * WIN] for n in range(2)]
        SPARE = STATE + 2 * WIN
        zeros = work[0:C, SPARE:SPARE + PAD * B]
        sel_i = work[0:KS, SPARE + PAD * B:SPARE + PAD * B + 2 * FEATS].bitcast(I32).rearrange("p (s n) -> p s n", s=2)
        spare = work[0:1, 2 * STATE - 1:2 * STATE]
        SPARE += PAD * B + 2 * FEATS
        unused = work[0:KC, SPARE:SPARE + CHUNK // 2].bitcast(BF16)
        wring = sb("wring", [P, RING, CHUNK], F32)
        signs = sb("signs", [P, 2, CHUNK], F16)
        bias_sb = [sb(f"bias{m}", [P, U * V], F32) for m in range(2)]
        gb_sb = sb("gb_sb", [P, 4], F32)
        mats_sb = sb("mats_sb", [P, 4, P], F32)
        in_quadrant, everywhere, same_channel, same_pair = (mats_sb[:, n, :] for n in range(4))
        stats = sb("stats", [P, 6, 512], F32)
        red = stats[:, 0:2, :]
        mean, rstd, tmp_a, tmp_b = (stats[:, n, :] for n in range(2, 6))
        PAIR = ROW // 2
        narrow_rstd = rstd[:, ROW:ROW + PAIR]
        x_front = tmp_b[:, 0:ROW]
        u_sums = stats[:, 0:2, :].rearrange("p s n -> p (s n)")
        u_squares = stats[:, 2:4, :].rearrange("p s n -> p (s n)")
        u_squared = [tmp_a[:, 0:ROW], tmp_b[:, 0:ROW]]
        abs_sums = sb("abs_sums", [P, 2 * U], F32)
        row_sums = sb("row_sums", [P, U * V], F32)
        square_sums = sb("square_sums", [P, U], F32)
        abs_sum = sb("abs_sum", [P, 1], F32)
        sc = sb("sc", [P, 32], F32)
        relu_sums = sb("relu_sums", [P, NCHUNK], F32)
        sel = sb("sel", [KS, 2, FEATS], F16)
        row_id = sb("row_id", [KS, 1], F32)
        own = sb("own", [ROWS[0], 2], F32)
        parts = work[0:KS, :].bitcast(F16).rearrange("p (g n) -> p g n", g=G)
        feats = [state_b[0:FP, n * FT * FCOL:(n + 1) * FT * FCOL].rearrange("p (t n) -> p t n", t=FT) for n in range(2)]
        BESIDE = 2 * FT * FCOL
        xn = state_b[:, BESIDE:BESIDE + PART]
        hi_lo = signs[:, 0, 0:2 * PART].rearrange("p (k n) -> p k n", k=2)
        left = state_b[0:FP, BESIDE + PART:BESIDE + PART + 2 * FCOL].rearrange("p (s n) -> p s n", s=2)

        psum = ctx.enter_context(nc.psum_tensor("psum", [P, 8, 512], F32))

        image = nc.dram_tensor("image", (C, PAD, PAD, B), I32, kind="Internal").ap()
        parts_dram = nc.dram_tensor("parts_dram", (G, W, 2, NPART, PART), F16, kind="Internal").ap()

        x_in = sems("x_in", NCHUNK)
        consts_in = sem("consts_in")
        mats_in = sem("mats_in")
        zeros_set = sem("zeros_set")
        border_in = sem("border_in")
        sel_made = sem("sel_made")
        w_in = sems("w_in", RING)
        signs_made = sem("signs_made")
        sums_cleared = sem("sums_cleared")
        abs_made = sem("abs_made")
        conv_done = sem("conv_done")
        bank_free = sem("bank_free")
        window_in = sems("window_in", 2)
        image_in = [sems(f"image_in{l}_", NCHUNK) for l in range(3)]
        squares = sems("squares", 4)
        gn_red = sems("gn_red", 4)
        gn_acc = sems("gn_acc", 4)
        gn_sums = sems("gn_sums", 4)
        xn_made = sems("xn_made", 4)
        hi_made = sems("hi_made", 3)
        norm_made = sems("norm_made", 3)
        state_done = sems("state_done", 4)
        abs_red = sems("abs_red", 2)
        abs_total = sems("abs_total", 2)
        rows_summed = sem("rows_summed")
        rows_squared = sem("rows_squared")
        u_row_squared = sem("u_row_squared")
        u_row_summed = sem("u_row_summed")
        tile_free = sems("tile_free", 2)
        bn_sums_in = sems("bn_sums_in", 2)
        bn_sums = sems("bn_sums", 2)
        bn_affine = sems("bn_affine", 2)
        relu_made = sems("relu_made", 2)
        masks_made = sems("masks_made", 2)
        masked = sems("masked", 2)
        relu_red = sems("relu_red", 2)
        relu_total = sems("relu_total", 2)
        inverse = sem("inverse")
        root = sem("root")
        dve_chain = sem("dve_chain")
        act_chain = sem("act_chain")
        transposed = sem("transposed")
        centred = sem("centred")
        hi_split = sem("hi_split")
        lo_split = sem("lo_split")
        parts_out = sem("parts_out")
        parts_in = sem("parts_in")
        first_part_in = sem("first_part_in")
        gathered = sem("gathered")
        left_made = sem("left_made")
        feats_made = sem("feats_made")
        mixed = sem("mixed")
        result_made = sem("result_made")
        out_sem = sem("out_sem")

        block = ctx.enter_context(nc.Block())

        states = [(state_a, state_b), (state_a, state_b), (state_b, state_a)]

        def rows(t, c):
            return t[:, c * CU * ROW:(c + 1) * CU * ROW]

        def one(j):
            return slice(j, j + 1) if isinstance(j, int) else bass.ds(j, 1)

        def load_part(queue, j, k, landed):
            queue.dma_start(parts[k * W:(k + 1) * W, :, bass.ds(j * PART, PART)],
                            parts_dram[:, :, min(k, 1), one(j), :].rearrange("g w o n -> w g (o n)")
                            ).then_inc(landed, 16)

        @block.sync
        def _(sp):
            def load_weights(layer, u, slot):
                if layer < 3:
                    sp.dma_start(wring[0:KC, slot, :], w_conv[layer][u]).then_inc(w_in[slot], 16)
                else:
                    sp.dma_start(wring[0:ROWS[0], slot, 0:POS * W], w_own[u]).then_inc(w_in[slot], 16)
                    sp.dma_start(wring[0:FP, slot, POS * W:W3CHUNK], w_pairs[u]).then_inc(w_in[slot], 16)

            def load_rows(n, u, taps=range(1, TAPS)):
                for tap in taps:
                    sp.dma_start(window[n][tap * C:(tap + 1) * C, :].bitcast(I32),
                                 image[:, bass.ds(u + tap, UC), :, :].rearrange("c u v b -> c (u v b)")
                                 ).then_inc(window_in[n], 16)

            for c in range(NCHUNK):
                sp.dma_start(rows(state_a, c), rows(x, c)).then_inc(x_in[c], 16)
            sp.dma_start(mats_sb[:, :, :], mats).then_inc(mats_in, 16)
            for s in range(RING):
                load_weights(0, s, s)
            sp.wait_ge(zeros_set, 1)
            zi = zeros.bitcast(I32)
            for edge in (0, PAD - 1):
                sp.dma_start(image[:, edge, :, :].rearrange("c v b -> c (v b)"), zi).then_inc(border_in, 16)
                sp.dma_start(image[:, 1:PAD - 1, edge, :],
                             zi[:, 0:U * B].rearrange("c (u b) -> c u b", u=U)).then_inc(border_in, 16)
            sp.wait_ge(border_in, 64)
            for layer in range(3):
                ni = norm.bitcast(I32).rearrange("p (u n) -> p u n", u=U)
                if layer:
                    for n in range(2):
                        sp.wait_ge(window_in[n], 16 * TAPS * 8 * layer)
                    sp.wait_ge(conv_done, U * layer)
                def slot_used(u):
                    if layer == 1:
                        sp.wait_ge(conv_done, U * layer + u + 1)
                    else:
                        sp.wait_ge(signs_made, U * (layer // 2) + u + 1)
                        sp.wait_ge(abs_made, U * (layer // 2) + u + 1)

                def next_weights(u, s):
                    slot_used(u)
                    load_weights(layer, u + RING, s)

                def next_rows(u, it, s):
                    sp.wait_ge(tile_free[s // 2], it + ((U // UC // 2 - 1) * layer + 1))
                    load_rows(s // 2, u + 1 + UC)

                if layer != 1:
                    next_weights(0, 0)
                for c in range(NCHUNK):
                    sp.wait_ge(norm_made[layer], c + 1)
                    for g in range(G):
                        sp.dma_start(image[:, 1 + c * CU:1 + (c + 1) * CU, 1 + g * V:1 + (g + 1) * V, :]
                                     .rearrange("c u v b -> c u (v b)"),
                                     ni[g * C:(g + 1) * C, c * CU:(c + 1) * CU, :]).then_inc(image_in[layer][c], 16)
                    if c < 2:
                        sp.wait_ge(image_in[layer][c], 16 * G)
                        load_rows(c, c * UC, range(c, TAPS))
                    if layer != 1 and c == ROWS_AFTER:
                        next_rows(1, 0, 1)
                    if layer != 1 and c in WEIGHTS_AFTER:
                        s = 1 + WEIGHTS_AFTER.index(c)
                        next_weights(s, s)
                for c in range(2, NCHUNK):
                    sp.wait_ge(image_in[layer][c], 16 * G)

                for s in range(RING):
                    if layer == 1:
                        next_weights(s, s)
                    if s == 3 or layer == 1 and s == 1:
                        next_rows(s, 0, s)
                with sp.Fori(1, U // RING - 1) as it:
                    for s in range(RING):
                        next_weights(it * RING + s, s)
                        if s % 2:
                            next_rows(it * RING + s, it, s)
                for s in range(RING):
                    slot_used(U - RING + s)
                    load_weights(layer + 1, s, s)

            sp.wait_ge(parts_out, 16)
            for k in range(2):
                load_part(sp, 0, k, first_part_in)

            def store_result(columns):
                sp.dma_start(out[:, columns], state_a[:, columns]).then_inc(out_sem, 16)

            with sp.Fori(0, NPART - 1) as j:
                for s in range(RING):
                    sp.wait_ge(result_made if s % 2 else mixed, j * RING + (s + 1))
                    load_weights(3, j * RING + (s + RING), s)
                    if s % 2:
                        store_result(bass.ds(j * PART + (s - 1) * C4 * B, 2 * C4 * B))
            for s in range(1, RING, 2):
                sp.wait_ge(result_made, NK - RING + s + 1)
                first = (NK - RING + s - 1) * C4 * B
                store_result(slice(first, first + 2 * C4 * B))
            sp.wait_ge(out_sem, 16 * NK // 2)

        @block.gpsimd
        def _(pool):
            pool.memset(zeros, 0.0).then_inc(zeros_set, 1)
            for n, (dst, src) in enumerate([(gb_sb[:, :], gamma_beta),
                                            (bias_sb[0][:, :], bias[0]), (bias_sb[1][:, :], bias[1]),
                                            (sel_i, sel_index), (row_id[:, :], sel_rows),
                                            (own[:, :], own_affine)]):
                pool.dma_start(dst, src).then_inc(consts_in, 16)
            tiles = U // UC // 2

            def copy_rows(n, other_done, reload=True):
                pool.wait_ge(window_in[1 - n], other_done)
                if reload:
                    pool.tensor_tensor(spare, zeros[0:1, 0:1], zeros[0:1, 0:1], ALU.add).then_inc(tile_free[n], 1)
                pool.tensor_copy(window[n][0:C, :], window[1 - n][(TAPS - 1) * C:KC, :]).then_inc(window_in[n], 16)

            for layer in range(3):
                copy_rows(1, 16 * TAPS * (tiles * layer + 1), reload=False)
                with pool.Fori(0, tiles - 1) as it:
                    for n in range(2):
                        pool.wait_ge(conv_done, it * RING + (U * layer + UC * (n + 1)))
                        copy_rows(n, it * (16 * TAPS) + 16 * TAPS * (tiles * layer + 1 + n))

            def store_part(j):
                pool.dma_start(parts_dram[:, :, :, one(j), :].rearrange("g w k o n -> (g w) k (o n)"),
                             hi_lo).then_inc(parts_out, 16)

            pool.wait_ge(lo_split, 1)
            store_part(0)
            pool.wait_ge(parts_out, 16)
            load_part(pool, 0, 2, parts_in)
            with pool.Fori(0, NPART - 1) as j:
                pool.wait_ge(lo_split, j + 2)
                store_part(j + 1)
                pool.wait_ge(parts_out, j * 16 + 32)
                for k in range(3):
                    load_part(pool, j + 1, k, parts_in)

        CONSTS = 16 * 6

        @block.scalar
        def _(act):
            chain = [0]

            def link(ins):
                chain[0] += 1
                ins.then_inc(act_chain, 1)

            def square(layer):
                st, scratch = states[layer]
                for c in range(NCHUNK):
                    if layer == 0:
                        act.wait_ge(x_in[c], 16)
                    else:
                        act.wait_ge(state_done[0], c + 1)
                    act.activation(rows(scratch, c), rows(st, c), ACT.Square).then_inc(squares[layer], 1)

            def take_root(out, inv, nth):
                act.wait_ge(inverse, nth)
                act.activation(out, inv, ACT.Sqrt).then_inc(root, 1)

            def signs_of(s):
                act.activation(signs[0:KC, s % 2, :], wring[0:KC, s, :], ACT.Sign).then_inc(signs_made, 1)

            def magnitudes(m, u, col, s, width):
                act.wait_ge(signs_made, u + U * m)
                return act.activation(unused[:, 0:width], wring[0:KC, s, CHUNK - width:CHUNK], ACT.Abs,
                                      accum_out=abs_sums[0:KC, col])

            def all_magnitudes(m, u):
                if u or m:
                    act.wait_ge(abs_made, U * m + u)
                act.activation(unused, wring[0:KC, u, :], ACT.Abs,
                               accum_out=abs_sums[0:KC, u:u + 1]).then_inc(abs_made, 1)

            for layer in range(3):
                st, scratch = states[layer]
                if layer < 2:
                    square(layer)
                if layer != 1:
                    for u in range(2):
                        act.wait_ge(w_in[u], 16 * (8 * layer + 1))
                        if layer:
                            act.wait_ge(conv_done, U * layer)
                        signs_of(u)
                if layer < 2:
                    take_root(narrow_rstd, tmp_a[:, 0:PAIR], 2 * layer + 1)
                else:
                    take_root(rstd, tmp_a, 4)
                if layer == 0:
                    act.wait_ge(sums_cleared, 1)
                if layer != 1:
                    all_magnitudes(layer // 2, 0)
                if layer == 1:
                    def square_u(u, s):
                        act.wait_ge(bank_free, u + (RING + U * layer + 1))
                        act.activation(u_squared[s], scratch[:, bass.ds(u * ROW, ROW)],
                                       ACT.Square).then_inc(u_row_squared, 1)

                    for s in range(2):
                        square_u(s, s)
                    with act.Fori(1, U // 2) as it:
                        for s in range(2):
                            act.wait_ge(u_row_summed, it * 2 + (s - 1))
                            square_u(it * 2 + s, s)
                    continue
                m = layer // 2
                hi = norm16.rearrange("p (u v k b) -> p u v k b", u=U, v=V, k=2)[:, :, :, 0, :]
                t = scratch[:, :].rearrange("p (u v b) -> p u v b", u=U, v=V)
                for c in range(NCHUNK):
                    act.wait_ge(xn_made[layer], c + 1)
                    us = slice(c * CU, (c + 1) * CU)
                    act.activation(hi[:, us], t[:, us], ACT.Copy).then_inc(hi_made[layer], 1)
                    if c < RING - 1:
                        act.wait_ge(w_in[c + 1], 16 * (8 * layer + 1))
                        all_magnitudes(m, c + 1)
                    if c in SIGNS_AFTER:
                        u = 2 + SIGNS_AFTER.index(c)
                        act.wait_ge(conv_done, U * layer + u - 1)
                        signs_of(u)

                def square_row(u, col):
                    if m or not isinstance(u, int) or u:
                        act.wait_ge(rows_squared, u + U * m)
                    act.wait_ge(bank_free, u + (RING + U * layer + 1))
                    act.activation(tmp_b[:, 0:ROW], scratch[:, bass.ds(u * ROW, ROW)], ACT.Square,
                                   accum_out=square_sums[:, col]).then_inc(rows_squared, 1)

                for u in range(RING - 2):
                    square_row(u, slice(u, u + 1))
                with act.Fori(1, U // RING) as it:
                    for s in range(RING):
                        act.wait_ge(w_in[s], it * 16 + 16 * (8 * layer + 1))
                        act.wait_ge(conv_done, it * RING + (U * layer + s - 1))
                        magnitudes(m, it * RING + s, bass.ds(it * RING + (U + s), 1), s, ACT_ABS)
                        signs_of(s)
                        square_row(it * RING + (s - 2), bass.ds(it * RING + (s - 2), 1))
                for u in range(U - 2, U):
                    square_row(u, slice(u, u + 1))
                take_root(sc[:, 11:12], sc[:, 15:16], 2 + 3 * m)
                for c in range(NCHUNK):
                    act.wait_ge(bn_affine[m], c + 1)
                    act.activation(rows(scratch, c), rows(scratch, c), ACT.Relu,
                                   accum_out=relu_sums[:, c:c + 1]).then_inc(relu_made[m], 1)
                for c in range(MASKS, NCHUNK):
                    act.wait_ge(relu_made[m], c + 1)
                    act.activation(rows(scratch, c), rows(scratch, c), ACT.Sign).then_inc(masks_made[m], 1)

            for i in range(V):
                act.wait_ge(transposed, i + 1)
                act.activation(norm[:, i * 1024:(i + 1) * 1024], state_a[:, i * 1024:(i + 1) * 1024],
                               ACT.Square).then_inc(squares[3], 1)
            take_root(rstd[:, 0:B], tmp_a[:, 0:B], 6)

            def high(j):
                act.wait_ge(xn_made[3], j + 1)
                act.activation(hi_lo[:, 0, :], xn, ACT.Copy).then_inc(hi_split, 1)

            def copy_left(k, parity, t):
                act.wait_ge(gathered, k * FT + (t + 1))
                n = (parity * FT + t) % 2
                if t == 0:
                    act.activation(left[0:ROWS[0], n, :], psum[0:ROWS[0], 2 + n, :], ACT.Identity,
                                   scale=own[:, 0:1], bias=own[:, 1:2]).then_inc(left_made, 1)
                else:
                    act.activation(left[:, n, :], psum[0:FP, 2 + n, :], ACT.Copy,
                                   scale=1.0 / HALF_SCALE / HALF_SCALE).then_inc(left_made, 1)

            high(0)
            for t in range(FT):
                copy_left(0, 0, t)
            with act.Fori(0, NPART - 1) as j:
                for s in range(RING):
                    for t in range(FT):
                        copy_left(j * RING + (s + 1), (s + 1) % 2, t)
                        if s == 0 and t == HIGH_AFTER:
                            act.wait_ge(parts_out, j * 16 + 16)
                            high(j + 1)
            for k in range(NK - RING + 1, NK):
                for t in range(FT):
                    copy_left(k, k % 2, t)

        @block.vector
        def _(dve):
            chain = [0]

            def link(ins):
                chain[0] += 1
                ins.then_inc(dve_chain, 1)
                dve.wait_ge(dve_chain, chain[0])

            def inverse_root(out, var, tmp, eps, nth):
                link(dve.tensor_scalar(var, var, eps, None, ALU.add))
                dve.reciprocal(tmp, var).then_inc(inverse, 1)
                dve.wait_ge(root, nth)
                link(dve.tensor_tensor(tmp, out, out, ALU.mult))
                link(dve.tensor_tensor(tmp, tmp, var, ALU.mult))
                link(dve.tensor_scalar(tmp, tmp, -0.5, 1.5, ALU.mult, ALU.add))
                link(dve.tensor_tensor(out, out, tmp, ALU.mult))

            dve.memset(sc[:, :], 0.0).then_inc(bank_free, RING)
            dve.memset(abs_sums[:, :], 0.0).then_inc(sums_cleared, 1)

            def pairs_of_v(t):
                return t.rearrange("p (u r) -> p r u", r=ROW)

            def pairs_of_u(t):
                return t.rearrange("p (u k b) -> p u b k", u=U // 2, b=B)

            for layer in range(3):
                st, scratch = states[layer]
                by_v = layer < 2
                if by_v:
                    half = U // 2 * ROW
                    if layer == 0:
                        for c in range(X_PIECES):
                            dve.wait_ge(x_in[c], 16)
                        dve.tensor_reduce(x_front, pairs_of_v(st[:, 0:X_PIECES * CU * ROW]), X, ALU.add).then_inc(gn_red[0], 1)
                    for h in range(2):
                        dve.wait_ge(squares[layer], NCHUNK // 2 * (h + 1))
                        dve.tensor_reduce(red[:, 1, h * ROW:(h + 1) * ROW],
                                          pairs_of_v(scratch[:, h * half:(h + 1) * half]), X, ALU.add
                                          ).then_inc(gn_red[layer], 1)
                    dve.wait_ge(gn_acc[layer], 1)
                    dve.tensor_copy(red[:, 0, 0:ROW], psum[:, 4, 0:ROW]).then_inc(gn_red[layer], 1)
                dve.wait_ge(gn_sums[layer], 1)
                if by_v:
                    def each(t):
                        return t[:, 0:PAIR].rearrange("p (q b) -> p q b", b=B)

                    def both(t):
                        return t[:, 0:ROW].rearrange("p (q t b) -> p q t b", t=2, b=B)

                    sums, sums2, ta, tb, rs = (each(t) for t in (psum[:, 5, :], psum[:, 6, :], tmp_a, tmp_b, narrow_rstd))
                    link(dve.tensor_scalar(both(mean), sums.unsqueeze(2).to_broadcast([P, V // 2, 2, B]),
                                           1.0 / GN_COUNT / C, None, ALU.mult))
                    mn = both(mean)[:, :, 0, :]
                else:
                    sums, sums2, mn, ta, tb, rs = psum[:, 5, :], psum[:, 6, :], mean, tmp_a, tmp_b, rstd
                    link(dve.tensor_scalar(mn, sums, 1.0 / GN_COUNT, None, ALU.mult))
                link(dve.tensor_tensor(ta, mn, mn, ALU.mult))
                link(dve.scalar_tensor_tensor(tb, sums2, 1.0 / GN_COUNT, ta, ALU.mult, ALU.subtract))
                inverse_root(rs, tb, ta, GN_EPS, 2 * layer + 1 - layer // 2)
                if by_v:
                    link(dve.tensor_scalar(both(rstd), rs.unsqueeze(2).to_broadcast([P, V // 2, 2, B]),
                                           1.0 if layer else HALF_SCALE, None, ALU.mult))
                else:
                    link(dve.tensor_scalar(rs, rs, HALF_SCALE, None, ALU.mult))
                mn, rs = (t[:, 0:ROW] if by_v else t for t in (mean, rstd))
                dst = norm if layer == 1 else scratch
                halves = norm16.rearrange("p (u v k b) -> p u v k b", u=U, v=V, k=2)
                t4 = scratch[:, :].rearrange("p (u v b) -> p u v b", u=U, v=V)
                for c in range(NCHUNK + 1):
                    if c < NCHUNK:
                        if by_v:
                            view = [rows(t, c).rearrange("p (u r) -> p u r", r=ROW) for t in (st, dst)]
                            m_op, r_op = (t.unsqueeze(1).to_broadcast([P, CU, ROW]) for t in (mn, rs))
                        else:
                            view = [rows(t, c).rearrange("p (u k b) -> p u k b", u=CU // 2, b=B) for t in (st, dst)]
                            m_op, r_op = (t[:, c * CU // 2 * B:(c + 1) * CU // 2 * B]
                                          .rearrange("p (u b) -> p u b", b=B)
                                          .unsqueeze(2).to_broadcast([P, CU // 2, 2 * V, B]) for t in (mn, rs))
                        link(dve.tensor_tensor(view[1], view[0], m_op, ALU.subtract))
                        dve.tensor_tensor(view[1], view[1], r_op, ALU.mult).then_inc(
                            norm_made[1] if layer == 1 else xn_made[layer], 1)
                    if c and layer != 1:
                        us = slice((c - 1) * CU, c * CU)
                        dve.wait_ge(xn_made[layer], c)
                        dve.wait_ge(hi_made[layer], c)
                        dve.tensor_tensor(halves[:, us, :, 1, :], t4[:, us], halves[:, us, :, 0, :],
                                          ALU.subtract).then_inc(norm_made[layer], 1)

                if layer == 0:
                    dve.wait_ge(consts_in, CONSTS)
                    for side in range(2):
                        dve.tensor_scalar(sel[:, side, :], sel_i[:, side, :], row_id[:, 0:1], None,
                                          ALU.is_equal).then_inc(sel_made, 1)

                if layer == 1:
                    src = st[:, :].rearrange("p (h v b) -> p h v b", h=H, b=B)
                    for wg in range(G):
                        with dve.Fori(0, V // RING) as half:
                            for s in range(RING):
                                dve.wait_ge(conv_done, half * RING + (U * layer + wg * V + s + 1))
                                for g in range(G):
                                    res = scratch[g * C:(g + 1) * C, bass.ds((half * RING + (wg * V + s)) * ROW, ROW)]
                                    old = src[wg * C:(wg + 1) * C, g * V:(g + 1) * V, bass.ds(half * RING + s, 1), :]
                                    last = dve.tensor_tensor(
                                        res.rearrange("p (v b) -> p v b", b=B),
                                        psum[g * C:(g + 1) * C, s % 2 * 2:s % 2 * 2 + 2, :].rearrange(
                                            "p k (v g b) -> p (k v) g b", g=G, b=B)[:, :, g, :],
                                        old.rearrange("p v o b -> p v (o b)"), ALU.add)
                                last.then_inc(bank_free, 1)
                                u = half * RING + (wg * V + s)
                                res = scratch[:, bass.ds(u * ROW, ROW)].rearrange("p (v b) -> p b v", b=B)
                                dve.wait_ge(bank_free, half * RING + (RING + U * layer + wg * V + s + 1))
                                dve.tensor_reduce(u_sums[:, bass.ds(u * B, B)], res, X, ALU.add)
                                dve.wait_ge(u_row_squared, half * RING + (wg * V + s + 1))
                                dve.tensor_reduce(u_squares[:, bass.ds(u * B, B)],
                                                  u_squared[s % 2].rearrange("p (v b) -> p b v", b=B),
                                                  X, ALU.add).then_inc(u_row_summed, 1)
                    continue

                m = layer // 2
                bias_sq = tmp_b[:, ROW:2 * ROW]
                dve.wait_ge(consts_in, CONSTS)
                link(dve.tensor_tensor(bias_sq, bias_sb[m][:, :], bias_sb[m][:, :], ALU.mult))
                link(dve.tensor_reduce(sc[:, 16:17], bias_sb[m][:, :], X, ALU.add))
                link(dve.tensor_reduce(sc[:, 17:18], bias_sq, X, ALU.add))

                def evacuate(u, s):
                    dve.wait_ge(conv_done, u + (U * layer + 1))
                    raw = scratch[:, bass.ds(u * ROW, ROW)].rearrange("p (v b) -> p v b", b=B)
                    dve.tensor_reduce(raw, psum[:, s, :].rearrange("p (v k b) -> p v b k", k=2, b=B), X,
                                      ALU.add).then_inc(bank_free, 1)
                    dve.wait_ge(bank_free, u + (RING + U * layer + 1))
                    dve.tensor_reduce(row_sums[:, bass.ds(u * V, V)], raw, X, ALU.add).then_inc(rows_summed, 1)

                for u in range(RING):
                    evacuate(u, u)
                with dve.Fori(1, U // RING) as it:
                    for s in range(RING):
                        dve.wait_ge(w_in[s], it * 16 + 16 * (8 * layer + 1))
                        dve.tensor_reduce(abs_sums[0:KC, bass.ds(it * RING + s, 1)], wring[0:KC, s, 0:CHUNK - ACT_ABS],
                                          X, ALU.add, apply_absolute_value=True).then_inc(abs_made, 1)
                        evacuate(it * RING + s, s)
                dve.wait_ge(abs_made, U * (m + 1))
                dve.wait_ge(signs_made, U * (m + 1))
                dve.tensor_reduce(abs_sum[0:KC, :], abs_sums[0:KC, :], X, ALU.add).then_inc(abs_red[m], 1)
                dve.wait_ge(rows_summed, U * (m + 1))
                link(dve.tensor_tensor(bias_sq, row_sums[:, :], bias_sb[m][:, :], ALU.mult))
                link(dve.tensor_reduce(sc[:, 18:19], bias_sq, X, ALU.add))
                link(dve.tensor_reduce(sc[:, 19:20], row_sums[:, :], X, ALU.add))
                dve.wait_ge(rows_squared, U * (m + 1))
                link(dve.tensor_reduce(sc[:, 20:21], square_sums[:, :], X, ALU.add))
                link(dve.tensor_scalar(sc[:, 21:22], sc[:, 18:19], 2.0, None, ALU.mult))
                link(dve.tensor_scalar(sc[:, 22:24], sc[:, 16:18], float(B), None, ALU.mult))
                dve.wait_ge(abs_total[m], 1)
                link(dve.tensor_scalar(sc[:, 0:1], psum[:, 4, 0:1], 1.0 / (KC * U * CHUNK) / HALF_SCALE, None, ALU.mult))
                link(dve.scalar_tensor_tensor(sc[:, 2:3], sc[:, 19:20], sc[:, 0:1], sc[:, 22:23], ALU.mult, ALU.add))
                link(dve.scalar_tensor_tensor(sc[:, 24:25], sc[:, 20:21], sc[:, 0:1], sc[:, 21:22], ALU.mult, ALU.add))
                dve.scalar_tensor_tensor(sc[:, 3:4], sc[:, 24:25], sc[:, 0:1], sc[:, 23:24], ALU.mult,
                                         ALU.add).then_inc(bn_sums_in[m], 1)
                dve.wait_ge(bn_sums[m], 1)
                link(dve.tensor_scalar(sc[:, 6:8], psum[:, 4, 8:10], 1.0 / BN_COUNT, None, ALU.mult))
                link(dve.tensor_tensor(sc[:, 8:9], sc[:, 6:7], sc[:, 6:7], ALU.mult))
                link(dve.tensor_tensor(sc[:, 10:11], sc[:, 7:8], sc[:, 8:9], ALU.subtract))
                inverse_root(sc[:, 11:12], sc[:, 10:11], sc[:, 15:16], BN_EPS, 2 + 3 * m)
                link(dve.tensor_tensor(sc[:, 4:5], sc[:, 11:12], gb_sb[:, 2 * m:2 * m + 1], ALU.mult))
                link(dve.tensor_tensor(sc[:, 12:13], sc[:, 4:5], sc[:, 6:7], ALU.mult))
                link(dve.tensor_tensor(sc[:, 5:6], gb_sb[:, 2 * m + 1:2 * m + 2], sc[:, 12:13], ALU.subtract))
                link(dve.tensor_tensor(sc[:, 25:26], sc[:, 4:5], sc[:, 0:1], ALU.mult))
                offset = tmp_b[:, 0:ROW]
                link(dve.tensor_scalar(offset, bias_sb[m][:, :], sc[:, 4:5], sc[:, 5:6], ALU.mult, ALU.add))
                for c in range(NCHUNK):
                    y = rows(scratch, c).rearrange("p (r b) -> p r b", b=B)
                    off = offset[:, c * CU * V:(c + 1) * CU * V].unsqueeze(2).to_broadcast([P, CU * V, B])
                    dve.scalar_tensor_tensor(y, y, sc[:, 25:26], off, ALU.mult, ALU.add).then_inc(bn_affine[m], 1)
                for c in range(MASKS):
                    dve.wait_ge(relu_made[m], c + 1)
                    dve.tensor_scalar(rows(scratch, c), rows(scratch, c), 0.0, None, ALU.is_gt).then_inc(masked[m], 1)
                dve.wait_ge(relu_made[m], NCHUNK)
                dve.tensor_reduce(sc[:, 13:14], relu_sums[:, :], X, ALU.add).then_inc(relu_red[m], 1)
                dve.wait_ge(relu_total[m], 1)
                link(dve.tensor_scalar(sc[:, 14:15], psum[:, 4, 24:25], 1.0 / (BN_COUNT * C), None, ALU.mult))
                for c in range(NCHUNK):
                    if c < MASKS:
                        dve.wait_ge(masked[m], c + 1)
                    else:
                        dve.wait_ge(masks_made[m], c - MASKS + 1)
                    dve.scalar_tensor_tensor(rows(st, c), rows(scratch, c), sc[:, 14:15], rows(st, c),
                                             ALU.mult, ALU.add).then_inc(state_done[layer], 1)

            dve.wait_ge(state_done[2], NCHUNK)
            old = state_b[:, :].rearrange("p (w i b) -> p i b w", w=W, b=B)
            for i in range(V):
                dve.transpose(state_a[:, i * 1024:(i + 1) * 1024].rearrange("p (c b) -> p b c", b=B),
                              old[:, i]).then_inc(transposed, 1)
            dve.wait_ge(transposed, V)
            dve.wait_ge(squares[3], V)
            dve.tensor_reduce(red[:, 1, 0:B], norm.rearrange("p (r b) -> p b r", b=B), X,
                              ALU.add).then_inc(gn_red[3], 1)
            dve.wait_ge(gn_acc[3], 1)
            link(dve.tensor_reduce(red[:, 0, 0:B], psum[:, 4, :].rearrange("p (c b) -> p b c", b=B), X, ALU.add))
            dve.wait_ge(gn_sums[3], 1)
            mn, rs, ta, tb = (t[:, 0:B] for t in (mean, rstd, tmp_a, tmp_b))
            link(dve.tensor_scalar(mn, red[:, 0, 0:B], 1.0 / GN_COUNT, None, ALU.mult))
            link(dve.tensor_tensor(ta, mn, mn, ALU.mult))
            link(dve.scalar_tensor_tensor(tb, psum[:, 5, 0:B], 1.0 / GN_COUNT, ta, ALU.mult, ALU.subtract))
            inverse_root(rs, tb, ta, GN_EPS, 6)
            link(dve.tensor_scalar(rs, rs, HALF_SCALE, None, ALU.mult))
            m_op, r_op = (t.unsqueeze(1).to_broadcast([P, PART // B, B]) for t in (mn, rs))

            def centre(j):
                dve.tensor_tensor(xn.rearrange("p (c b) -> p c b", b=B),
                                  state_a[:, bass.ds(j * PART, PART)].rearrange("p (c b) -> p c b", b=B),
                                  m_op, ALU.subtract).then_inc(centred, 1)

            def scale(j):
                dve.wait_ge(centred, j + 1)
                t = xn.rearrange("p (c b) -> p c b", b=B)
                dve.tensor_tensor(t, t, r_op, ALU.mult).then_inc(xn_made[3], 1)

            def low(j):
                dve.wait_ge(xn_made[3], j + 1)
                dve.wait_ge(hi_split, j + 1)
                dve.tensor_tensor(hi_lo[:, 1, :], xn, hi_lo[:, 0, :], ALU.subtract).then_inc(lo_split, 1)

            centre(0)
            scale(0)
            low(0)

            def product(k, n, t):
                dve.wait_ge(left_made, k * FT + (t + 1))
                q, bank = slice(0, ROWS[t]), (n * FT + t) % 2
                dve.tensor_tensor(feats[n][q, t, :], psum[q, (4 if t else 2) + bank, :], left[q, bank, :],
                                  ALU.mult).then_inc(feats_made, 1)

            def add_result(k, n):
                dve.wait_ge(mixed, k + 1)
                res = state_a[:, bass.ds(k * 128, 128)]
                for g in range(G):
                    q = slice(g * C, (g + 1) * C)
                    out_g = res[q, :].rearrange("p (c b) -> p c b", b=B)
                    last = dve.tensor_tensor(
                        out_g, psum[q, 6 + n, :].rearrange("p (c g b) -> p c g b", g=G, b=B)[:, :, g, :], out_g, ALU.add)
                last.then_inc(result_made, 1)

            for t in range(FT):
                product(0, 0, t)
            product(1, 1, 0)
            with dve.Fori(0, NPART - 1) as j:
                for s in range(RING):
                    for t in range(1, FT):
                        product(j * RING + (s + 1), (s + 1) % 2, t)
                        for step, after in ((centre, CENTRE_AFTER), (scale, SCALE_AFTER), (low, LOW_AFTER)):
                            if s == 0 and t == after:
                                step(j + 1)
                    product(j * RING + (s + 2), s % 2, 0)
                    add_result(j * RING + s, s % 2)
            for s in range(RING):
                k = NK - RING + s
                if k + 1 < NK:
                    for t in range(1, FT):
                        product(k + 1, (s + 1) % 2, t)
                if k + 2 < NK:
                    product(k + 2, s % 2, 0)
                add_result(k, s % 2)

        @block.tensor
        def _(pe):
            pe.wait_ge(mats_in, 16)
            for layer in range(3):
                st, scratch = states[layer]
                by_v = layer < 2
                if by_v:
                    first = 0 if layer else X_PIECES * CU
                    for u in range(first, U):
                        if u % CU == 0:
                            if layer:
                                pe.wait_ge(state_done[0], u // CU + 1)
                            else:
                                pe.wait_ge(x_in[u // CU], 16)
                        last = pe.matmul(psum[:, 4, 0:ROW], in_quadrant, st[:, u * ROW:(u + 1) * ROW],
                                         start=(u == first), stop=(layer == 1 and u == U - 1))
                    if layer == 0:
                        pe.wait_ge(gn_red[0], 1)
                        last = pe.matmul(psum[:, 4, 0:ROW], in_quadrant, x_front, start=False, stop=True)
                    last.then_inc(gn_acc[layer], 1)
                    pe.wait_ge(gn_red[layer], 4 if layer == 0 else 3)
                    for side in range(2):
                        views = [red[:, side, h * ROW:(h + 1) * ROW].rearrange("p (q t b) -> p q t b", t=2, b=B)[:, :, t, :]
                                 for h in range(side + 1) for t in range(2)]
                        for n, r in enumerate(views):
                            last = pe.matmul(psum[:, 5 + side, 0:PAIR], in_quadrant, r,
                                             start=(n == 0), stop=(n == len(views) - 1))
                else:
                    early = U // 2 - 2
                    for pairs, need in ((slice(0, early), 2 * early), (slice(early, U // 2), U)):
                        pe.wait_ge(u_row_summed, need)
                        for side in range(2):
                            for t in range(2):
                                r = (u_sums, u_squares)[side].rearrange("p (u t b) -> p u t b", t=2, b=B)[:, pairs, t, :]
                                last = pe.matmul(psum[:, 5 + side, pairs.start * B:pairs.stop * B], everywhere, r,
                                                 start=(t == 0), stop=(t == 1))
                last.then_inc(gn_sums[layer], 1)

                binary = layer != 1
                cols = 2 * B if binary else B
                with pe.Fori(0, U // RING) as it:
                    for s in range(RING):
                        if s % UC == 0:
                            pe.wait_ge(window_in[s // UC], it * (16 * TAPS) + 16 * TAPS * (8 * layer + 1))
                        if binary:
                            pe.wait_ge(signs_made, it * RING + (U * (layer // 2) + s + 1))
                            wt = signs[0:KC, s % 2, :]
                        else:
                            pe.wait_ge(w_in[s], it * 16 + 16 * (8 * layer + 1))
                            wt = wring[0:KC, s, :]
                        win = window[s // UC].bitcast(F16) if binary else window[s // UC]
                        win = win.rearrange("p (u v n) -> p u v n", u=UC, v=PAD)[:, s % UC, :, :]
                        if binary:
                            wt = wt.rearrange("p (v g t o) -> p v g t o", v=V, g=G, t=TAPS)
                            pe.wait_ge(bank_free, it * RING + (U * layer + s + 1))
                            for v in range(V):
                                for t in range(TAPS):
                                    for g in range(G):
                                        last = pe.matmul(psum[g * C:(g + 1) * C, s, v * cols:(v + 1) * cols],
                                                         wt[:, v, g, t, :], win[:, g * V + v + t, :],
                                                         start=(v == 0 and t == 0), stop=(v == V - 1 and t == TAPS - 1),
                                                         skip_group_check=True)
                        else:
                            wt = wt.rearrange("p (v t m) -> p v t m", v=V, t=TAPS)
                            pe.wait_ge(bank_free, it * RING + (RING + U * layer + s - 1))
                            for v in range(V):
                                for t in range(TAPS):
                                    bank = s % 2 * 2 + v // (V // 2)
                                    col = v % (V // 2) * G * cols
                                    last = pe.matmul(psum[:, bank, col:col + G * cols], wt[:, v, t, :],
                                                     win[:, v + t:v + t + (G - 1) * V + 1:V, :],
                                                     start=(v % (V // 2) == 0 and t == 0),
                                                     stop=(v % (V // 2) == V // 2 - 1 and t == TAPS - 1),
                                                     skip_group_check=True)
                        last.then_inc(conv_done, 1)
                if not binary:
                    continue
                m = layer // 2
                pe.wait_ge(abs_red[m], 1)
                pe.matmul(psum[:, 4, 0:1], everywhere[0:KC, :], abs_sum[0:KC, :], start=True, stop=True).then_inc(abs_total[m], 1)
                pe.wait_ge(bn_sums_in[m], 1)
                pe.matmul(psum[:, 4, 8:10], same_channel, sc[:, 2:4], start=True, stop=True).then_inc(bn_sums[m], 1)
                pe.wait_ge(relu_red[m], 1)
                pe.matmul(psum[:, 4, 24:25], everywhere, sc[:, 13:14], start=True, stop=True).then_inc(relu_total[m], 1)

            for i in range(V):
                pe.wait_ge(transposed, i + 1)
                for h in range(2):
                    last = pe.matmul(psum[:, 4, :], same_pair, state_a[:, (2 * i + h) * 512:(2 * i + h + 1) * 512],
                                     start=(i == 0 and h == 0), stop=(i == V - 1 and h == 1))
            last.then_inc(gn_acc[3], 1)
            pe.wait_ge(gn_red[3], 1)
            pe.matmul(psum[:, 5, 0:B], same_pair, red[:, 1, 0:B], start=True, stop=True).then_inc(gn_sums[3], 1)
            pe.wait_ge(sel_made, 2)

            def gather(k, n, t):
                cols = parts[:, :, bass.ds(k * (C4 * B), C4 * B)]
                bank = (n * FT + t) % 2
                for side in range(2 if t else 1):
                    last = pe.matmul(psum[0:ROWS[t], 2 + 2 * side + bank, :], sel[:, side, COLS[t]:COLS[t] + ROWS[t]], cols,
                                     start=True, stop=True)
                last.then_inc(gathered, 1)

            def mix(k, n, slot, t):
                pe.wait_ge(feats_made, k * FT + (t + 1))
                wt = wring[0:ROWS[t], slot, 0:W3CHUNK].rearrange("p (t c m) -> p t c m", t=FT, c=C4)
                f = feats[n][0:ROWS[t], t, :].rearrange("p (g c b) -> p c g b", g=G, c=C4)
                for c in range(C4):
                    last = pe.matmul(psum[:, 6 + n, c * G * B:(c + 1) * G * B], wt[:, t, c, :], f[:, c, :, :],
                                     start=(t == 0 and c == 0), stop=(t == FT - 1 and c == C4 - 1),
                                     skip_group_check=True)
                if t == FT - 1:
                    last.then_inc(mixed, 1)

            def step(k, s, fill, ahead=True):
                n = s % 2
                pe.wait_ge(w_in[s], fill)
                for t in range(FT):
                    if ahead:
                        pe.wait_ge(feats_made, k * FT + (FT + t - 1))
                        gather(k + 1, 1 - n, t)
                    mix(k, n, s, t)

            pe.wait_ge(first_part_in, 32)
            pe.wait_ge(parts_in, 16)
            for t in range(FT):
                if t >= 2:
                    pe.wait_ge(feats_made, t - 1)
                gather(0, 0, t)
            with pe.Fori(0, NPART - 1) as j:
                for s in range(RING):
                    if s == RING - 1:
                        pe.wait_ge(parts_in, j * 48 + 64)
                    step(j * RING + s, s, j * 32 + (16 * 3 * U // RING + 32))
            for s in range(RING):
                k = NK - RING + s
                step(k, s, (16 * 3 * U + 32 * NK) // RING, k < NK - 1)


def _rearranged(np, inputs):
    x = inputs["x"]
    xs = x.reshape(B, C, H, G, V).transpose(3, 1, 2, 4, 0).reshape(P, STATE)
    w0 = inputs["L0_conv_weight"].reshape(C, C, H, G, V, TAPS, TAPS)
    w0 = w0.transpose(2, 5, 1, 4, 3, 6, 0).reshape(U, KC, CHUNK)
    w1 = inputs["L1_conv_weights"].reshape(G, V, W, C, C, TAPS, TAPS)
    w1 = w1.transpose(2, 5, 4, 1, 6, 0, 3).reshape(U, KC, CHUNK)
    w2 = inputs["L2_conv_weight"].reshape(C, C, G, V, W, TAPS, TAPS)
    w2 = w2.transpose(4, 6, 1, 3, 2, 5, 0).reshape(U, KC, CHUNK)
    b0 = inputs["L0_conv_bias_p"].reshape(C, H, G, V).transpose(2, 0, 1, 3).reshape(P, U * V)
    b2 = inputs["L2_conv_bias_p"].reshape(C, G, V, W).transpose(1, 0, 3, 2).reshape(P, U * V)
    gb = np.stack([np.tile(inputs[n], G) for n in
                   ("L0_conv_gamma", "L0_conv_beta", "L2_conv_gamma", "L2_conv_beta")], axis=1)
    w3 = inputs["L3_conv_weight"].reshape(C // C4, C4, G, V, FEATS, W)
    own3 = w3[..., :2 * W, :].transpose(3, 0, 4, 1, 2, 5).reshape(NK, 2 * W, POS * W)
    pairs3 = w3[..., 2 * W:, :].reshape(C // C4, C4, G, V, PT, FP, W)
    pairs3 = pairs3.transpose(3, 0, 5, 4, 1, 2, 6).reshape(NK, FP, PT * POS * W)
    p = np.arange(P)
    mats = np.stack([p[:, None] // C == p // C, np.ones((P, P), bool), p[:, None] % C == p % C,
                     p[:, None] % C // 2 == p % C // 2], axis=1).astype(np.float32)
    own = np.arange(W, dtype=np.int32)
    left = np.concatenate([own, own, inputs["L3_conv_idx_a"].astype(np.int32)])
    right = np.concatenate([own, own, inputs["L3_conv_idx_b"].astype(np.int32)])
    index = np.broadcast_to(np.stack([left, right])[None], (KS, 2, FEATS))
    row = np.where(np.arange(KS) < 2 * W, np.arange(KS) % W, 2 * W).astype(np.float32)[:, None]
    affine = np.repeat(np.array([[0, 1 / HALF_SCALE], [1 / HALF_SCALE ** 2, 0]], np.float32), W, axis=0)
    return {"x": xs, "w0": w0, "w1": w1, "w2": w2, "b0": b0, "b2": b2, "gb": gb, "own3": own3, "pairs3": pairs3, "mats": mats,
            "row": row, "index": index, "affine": affine}


def kernel(**inputs):
    import numpy as np
    import concourse.bacc as bacc
    from concourse.bass_utils import run_bass_kernel_spmd as run

    arrays = {k: np.ascontiguousarray(v) for k, v in
              _rearranged(np, {k: np.asarray(v) for k, v in inputs.items()}).items()}
    nc = bacc.Bacc("TRN2", target_bir_lowering=False, num_devices=1)
    a = {k: nc.dram_tensor(f"in_{k}", v.shape, mybir.dt.from_np(v.dtype), kind="ExternalInput").ap()
         for k, v in arrays.items()}
    out = nc.dram_tensor("out_0", (P, STATE), F32, kind="ExternalOutput").ap()
    build(nc, a["x"], [a["w0"], a["w1"], a["w2"]], [a["b0"], a["b2"]], a["gb"], a["own3"], a["pairs3"], a["mats"], a["row"],
          a["index"], a["affine"], out)
    r = run(nc, [{f"in_{k}": v for k, v in arrays.items()}], core_ids=[0])
    got = r.results[0]["out_0"].reshape(G, W, V, C, B)
    return np.ascontiguousarray(got.transpose(4, 3, 0, 2, 1).reshape(B, C, H, W))
```
